# Optimizing a Trainium2 kernel written in Bass

```python
import numpy as np
import jax
import jax.numpy as jnp

def _softmax(x, axis=-1):
    return jax.nn.softmax(x, axis=axis)

def _gelu(x):
    return jax.nn.gelu(x, approximate=True)

def _silu(x):
    return jax.nn.silu(x)

def _sigmoid(x):
    return jax.nn.sigmoid(x)

def _layernorm(x, axis=-1, eps=1e-05):
    m = jnp.mean(x, axis=axis, keepdims=True)
    v = jnp.var(x, axis=axis, keepdims=True)
    return (x - m) / jnp.sqrt(v + eps)

def _scatter_add(tgt, idx, src, axis=0):
    return tgt.at[idx].add(src)

def _segment_sum(src, seg, n):
    return jax.ops.segment_sum(src, seg, n)
kernel_name = 'mk_prb_d2_jaxref_r8_de6dc4'

def setup_inputs(seed: int=0):
    np.random.seed(seed)
    _w = jnp.asarray

    def _L0_attn_setup():
        import jax, jax.numpy as jnp
        import numpy as np
        HEADS = 32
        key = jax.random.key(seed)
        ks = jax.random.split(key, 5)
        H = 512
        B, S = (2, 256)
        w_scale = 1.0 / np.sqrt(H)
        return {'x': jax.random.normal(ks[0], (B, S, H), dtype=jnp.float32), 'attn_qkvw': jax.random.normal(ks[1], (H, 3 * H), dtype=jnp.float32) * w_scale, 'attn_qkvb': jax.random.normal(ks[2], (3 * H,), dtype=jnp.float32) * 0.02, 'attn_ow': jax.random.normal(ks[3], (H, H), dtype=jnp.float32) * w_scale, 'attn_ob': jax.random.normal(ks[4], (H,), dtype=jnp.float32) * 0.02}
    _L0_attn_in = _L0_attn_setup()

    def _L0_ffn_setup():
        import jax, jax.numpy as jnp
        import numpy as np

        def sparsemax(z):
            E = z.shape[-1]
            z_sorted = -jnp.sort(-z, axis=-1)
            z_cum = jnp.cumsum(z_sorted, axis=-1)
            k = jnp.arange(1, E + 1, dtype=z.dtype)
            support = 1.0 + k * z_sorted > z_cum
            k_z = jnp.sum(support, axis=-1, keepdims=True)
            tau_sum = jnp.take_along_axis(z_cum, k_z.astype(jnp.int32) - 1, axis=-1)
            tau = (tau_sum - 1.0) / k_z.astype(z.dtype)
            return jnp.maximum(z - tau, 0.0)
        key = jax.random.key(seed)
        ks = jax.random.split(key, 6)
        B, S, D_IN, D_OUT, E, R = (8, 256, 512, 512, 8, 16)
        x = jax.random.normal(ks[0], (B, S, D_IN), dtype=jnp.float32)
        W_base = jax.random.normal(ks[1], (D_OUT, D_IN), dtype=jnp.float32) * D_IN ** (-0.5)
        b_base = jax.random.normal(ks[2], (D_OUT,), dtype=jnp.float32) * 0.01
        W_router = jax.random.normal(ks[3], (E, D_IN), dtype=jnp.float32) * D_IN ** (-0.5)
        b_router = jnp.zeros((E,), dtype=jnp.float32)
        lora_A = jax.random.normal(ks[4], (E, D_IN, R), dtype=jnp.float32) * D_IN ** (-0.5)
        lora_B = jnp.zeros((E, R, D_OUT), dtype=jnp.float32)
        return {'x': x, 'W_base': W_base, 'b_base': b_base, 'W_router': W_router, 'b_router': b_router, 'lora_A': lora_A, 'lora_B': lora_B}
    _L0_ffn_in = _L0_ffn_setup()

    def _L1_attn_setup():
        import jax, jax.numpy as jnp
        import numpy as np
        import math
        B, L, D, H = (32, 64, 512, 32)
        HD = D // H
        key = jax.random.key(seed)
        ks = jax.random.split(key, 9)
        s = 1.0 / math.sqrt(D)
        return {'x': jax.random.normal(ks[0], (B, L, D), jnp.float32), 'Wq': jax.random.normal(ks[1], (D, D), jnp.float32) * s, 'bq': jax.random.normal(ks[2], (D,), jnp.float32) * s, 'Wk': jax.random.normal(ks[3], (D, D), jnp.float32) * s, 'bk': jax.random.normal(ks[4], (D,), jnp.float32) * s, 'Wv': jax.random.normal(ks[5], (D, D), jnp.float32) * s, 'bv': jax.random.normal(ks[6], (D,), jnp.float32) * s, 'Wo': jax.random.normal(ks[7], (D, D), jnp.float32) * s, 'bo': jax.random.normal(ks[8], (D,), jnp.float32) * s}
    _L1_attn_in = _L1_attn_setup()

    def _L1_ffn_setup():
        import jax, jax.numpy as jnp
        import numpy as np
        B_L, B_H = (4, 8)
        LIN_SLOPE, LIN_INTER, EST_T = (1.0, 0.0, 64.0)
        BATCH, SEQ, IN_F, OUT_F = (4, 256, 512, 512)
        MAX_BITS = 8

        def dequant_kbit(qweight, lut, bit):
            O, I32 = (qweight.shape[1], qweight.shape[2])
            shifts = jnp.arange(32, dtype=jnp.int32)
            idx = jnp.zeros((O, I32 * 32), dtype=jnp.int32)
            for p in range(bit):
                bits = (qweight[p][:, :, None] >> shifts & 1).reshape(O, I32 * 32)
                idx = idx | bits << p
            return jnp.take_along_axis(lut, idx, axis=1)
        key = jax.random.key(seed)
        k = jax.random.split(key, 5)
        x = jax.random.normal(k[0], (BATCH, SEQ, IN_F), dtype=jnp.float32)
        qweight = jax.random.randint(k[1], (MAX_BITS, OUT_F, IN_F // 32), 0, 2147483647, dtype=jnp.int32)
        lut4 = jax.random.normal(k[2], (OUT_F, 2 ** B_L), dtype=jnp.float32) * 0.02
        lut8 = jax.random.normal(k[3], (OUT_F, 2 ** B_H), dtype=jnp.float32) * 0.02
        bias = jax.random.normal(k[4], (OUT_F,), dtype=jnp.float32) * 0.01
        return {'x': x, 'qweight': qweight, 'lut4': lut4, 'lut8': lut8, 'bias': bias}
    _L1_ffn_in = _L1_ffn_setup()
    _d = {'L0_attn_x': _L0_attn_in['x'], 'L0_attn_attn_qkvw': _L0_attn_in['attn_qkvw'], 'L0_attn_attn_qkvb': _L0_attn_in['attn_qkvb'], 'L0_attn_attn_ow': _L0_attn_in['attn_ow'], 'L0_attn_attn_ob': _L0_attn_in['attn_ob'], 'L0_ffn_W_base': _L0_ffn_in['W_base'], 'L0_ffn_b_base': _L0_ffn_in['b_base'], 'L0_ffn_W_router': _L0_ffn_in['W_router'], 'L0_ffn_b_router': _L0_ffn_in['b_router'], 'L0_ffn_lora_A': _L0_ffn_in['lora_A'], 'L0_ffn_lora_B': _L0_ffn_in['lora_B'], 'L1_attn_Wq': _L1_attn_in['Wq'], 'L1_attn_bq': _L1_attn_in['bq'], 'L1_attn_Wk': _L1_attn_in['Wk'], 'L1_attn_bk': _L1_attn_in['bk'], 'L1_attn_Wv': _L1_attn_in['Wv'], 'L1_attn_bv': _L1_attn_in['bv'], 'L1_attn_Wo': _L1_attn_in['Wo'], 'L1_attn_bo': _L1_attn_in['bo'], 'L1_ffn_qweight': _L1_ffn_in['qweight'], 'L1_ffn_lut4': _L1_ffn_in['lut4'], 'L1_ffn_lut8': _L1_ffn_in['lut8'], 'L1_ffn_bias': _L1_ffn_in['bias']}
    _x0 = _d['L0_attn_x']
    _d['L0_attn_x'] = jax.random.normal(jax.random.fold_in(jax.random.key(seed), 1), (2, 1024, 512), dtype=_x0.dtype)
    del _x0
    return _d

def reference(L0_attn_x, L0_attn_attn_qkvw, L0_attn_attn_qkvb, L0_attn_attn_ow, L0_attn_attn_ob, L0_ffn_W_base, L0_ffn_b_base, L0_ffn_W_router, L0_ffn_b_router, L0_ffn_lora_A, L0_ffn_lora_B, L1_attn_Wq, L1_attn_bq, L1_attn_Wk, L1_attn_bk, L1_attn_Wv, L1_attn_bv, L1_attn_Wo, L1_attn_bo, L1_ffn_qweight, L1_ffn_lut4, L1_ffn_lut8, L1_ffn_bias):

    def _L0_attn_ref(x, attn_qkvw, attn_qkvb, attn_ow, attn_ob):
        import jax, jax.numpy as jnp
        import numpy as np
        HEADS = 32
        B, S, H = x.shape
        hd = H // HEADS
        scale = 1.0 / np.sqrt(hd)
        qkv = x @ attn_qkvw + attn_qkvb
        qkv = qkv.reshape(B, S, 3, HEADS, hd)
        q = jnp.transpose(qkv[:, :, 0], (0, 2, 1, 3))
        k = jnp.transpose(qkv[:, :, 1], (0, 2, 1, 3))
        v = jnp.transpose(qkv[:, :, 2], (0, 2, 1, 3))
        scores = jnp.einsum('bhqd,bhkd->bhqk', q, k) * scale
        probs = jax.nn.softmax(scores, axis=-1)
        ctx = jnp.einsum('bhqk,bhkd->bhqd', probs, v)
        ctx = jnp.transpose(ctx, (0, 2, 1, 3)).reshape(B, S, H)
        return ctx @ attn_ow + attn_ob

    def _L0_ffn_ref(x, W_base, b_base, W_router, b_router, lora_A, lora_B):
        import jax, jax.numpy as jnp
        import numpy as np

        def sparsemax(z):
            E = z.shape[-1]
            z_sorted = -jnp.sort(-z, axis=-1)
            z_cum = jnp.cumsum(z_sorted, axis=-1)
            k = jnp.arange(1, E + 1, dtype=z.dtype)
            support = 1.0 + k * z_sorted > z_cum
            k_z = jnp.sum(support, axis=-1, keepdims=True)
            tau_sum = jnp.take_along_axis(z_cum, k_z.astype(jnp.int32) - 1, axis=-1)
            tau = (tau_sum - 1.0) / k_z.astype(z.dtype)
            return jnp.maximum(z - tau, 0.0)
        base_out = jnp.einsum('bsd,od->bso', x, W_base) + b_base
        logits = jnp.einsum('bsd,ed->bse', x, W_router) + b_router
        weights = sparsemax(logits)
        h = jnp.einsum('bsd,edr->bser', x, lora_A)
        expert_out = jnp.einsum('bser,bse,ero->bso', h, weights, lora_B)
        return base_out + expert_out

    def _L1_attn_ref(x, Wq, bq, Wk, bk, Wv, bv, Wo, bo):
        import jax, jax.numpy as jnp
        import numpy as np
        import math
        B, L, D, H = (32, 64, 512, 32)
        HD = D // H
        b, l, d = x.shape
        h, hd = (H, HD)
        q = (x @ Wq.T + bq).reshape(b, l, h, hd).transpose(0, 2, 1, 3)
        k = (x @ Wk.T + bk).reshape(b, l, h, hd).transpose(0, 2, 1, 3)
        v = (x @ Wv.T + bv).reshape(b, l, h, hd).transpose(0, 2, 1, 3)
        scores = jnp.einsum('bhqd,bhkd->bhqk', q, k) / math.sqrt(hd)
        causal = jnp.tril(jnp.ones((l, l), bool))
        scores = jnp.where(causal, scores, -jnp.inf)
        att = jax.nn.softmax(scores, axis=-1)
        out = jnp.einsum('bhqk,bhkd->bhqd', att, v)
        out = out.transpose(0, 2, 1, 3).reshape(b, l, d)
        return out @ Wo.T + bo

    def _L1_ffn_ref(x, qweight, lut4, lut8, bias):
        import jax, jax.numpy as jnp
        import numpy as np
        B_L, B_H = (4, 8)
        LIN_SLOPE, LIN_INTER, EST_T = (1.0, 0.0, 64.0)
        BATCH, SEQ, IN_F, OUT_F = (4, 256, 512, 512)
        MAX_BITS = 8

        def dequant_kbit(qweight, lut, bit):
            O, I32 = (qweight.shape[1], qweight.shape[2])
            shifts = jnp.arange(32, dtype=jnp.int32)
            idx = jnp.zeros((O, I32 * 32), dtype=jnp.int32)
            for p in range(bit):
                bits = (qweight[p][:, :, None] >> shifts & 1).reshape(O, I32 * 32)
                idx = idx | bits << p
            return jnp.take_along_axis(lut, idx, axis=1)
        e = jnp.linalg.norm(x, axis=-1) * LIN_SLOPE + LIN_INTER
        mask = e > EST_T
        w_l = dequant_kbit(qweight, lut4, B_L)
        w_h = dequant_kbit(qweight, lut8, B_H)
        y_l = jnp.einsum('bsi,oi->bso', x, w_l)
        y_h = jnp.einsum('bsi,oi->bso', x, w_h)
        y = jnp.where(mask[..., None], y_h, y_l) + bias
        return y
    x = L0_attn_x
    xn = _layernorm(x, axis=-1)
    x = x + _L0_attn_ref(xn, L0_attn_attn_qkvw, L0_attn_attn_qkvb, L0_attn_attn_ow, L0_attn_attn_ob) + _L0_ffn_ref(xn, L0_ffn_W_base, L0_ffn_b_base, L0_ffn_W_router, L0_ffn_b_router, L0_ffn_lora_A, L0_ffn_lora_B)
    xn = _layernorm(x, axis=-1)
    x = x + _L1_attn_ref(xn, L1_attn_Wq, L1_attn_bq, L1_attn_Wk, L1_attn_bk, L1_attn_Wv, L1_attn_bv, L1_attn_Wo, L1_attn_bo) + _L1_ffn_ref(xn, L1_ffn_qweight, L1_ffn_lut4, L1_ffn_lut8, L1_ffn_bias)
    return x

_drawn_inputs = setup_inputs


def setup_inputs(seed=0):
    import zlib

    import numpy as np

    out = dict(_drawn_inputs(seed))
    spreads = {'L0_ffn_b_router': (0.0, 0.53), 'L0_ffn_lora_B': (0.0, 0.1)}
    factors = {'L0_attn_attn_qkvb': 3.741,
     'L0_attn_attn_ob': 3.762,
     'L0_ffn_b_base': 7.635,
     'L1_attn_bq': 8.0,
     'L1_attn_bk': 8.0,
     'L1_ffn_bias': 8.0}
    for name, (base, spread) in spreads.items():
        noise = np.random.default_rng([zlib.crc32(name.encode()), seed]).standard_normal(out[name].shape)
        drawn = base * np.exp(spread * noise) if base else spread * noise
        out[name] = jnp.asarray(drawn.astype(out[name].dtype))
    for name, factor in factors.items():
        out[name] = (out[name] * factor).astype(out[name].dtype)
    return out
```

```python
from contextlib import ExitStack

import numpy as np

import concourse.bass as bass
from concourse import mybir

F32 = mybir.dt.float32
BF16 = mybir.dt.bfloat16
I32 = mybir.dt.int32
ALU = mybir.AluOpType
ACT = mybir.ActivationFunctionType
AX = mybir.AxisListType.X

P = 128
BATCH, SEQ, DIM = 2, 1024, 512
HEADS, HD = 32, 16
TOK = BATCH * SEQ
KT = DIM // P
CHUNK = 512
TT = CHUNK // P
NCH = SEQ // CHUNK
CHUNKS = BATCH * NCH
QUAD = 4
QUADS = HEADS // QUAD
STEPS = BATCH * QUADS
VW = 2 * HD
PARTS = 3
Q_ROWS = (0, 0, 0, 1, 1, 2)
K_ROWS = (0, 1, 2, 0, 1, 0)
SROWS = len(Q_ROWS) * HD
BROWS = SROWS + 2
QT = SEQ // P
QHS = SEQ // CHUNK
EXPERTS, RANK = 8, 16
NSTAGE = 3
QKT = 2 * DIM // P
PLANES, WORDS, BITS = 8, 16, 32
GO = 8
NIB = 16
POS = 4
LOADS = len(Q_ROWS) + len(K_ROWS) + 1
DMA = 16
EPS = 1e-5
SCALE = 1.0 / float(np.sqrt(HD))
MASKED = -1e38
NORM_T = 64.0

C_ID = 0
C_SEL = C_ID + P
C_KCOL = C_SEL + POS * 32
C_KARR = C_KCOL + 1
C_UP = C_KARR + EXPERTS
C_LO = C_UP + P
C_ALL = C_LO + P


def constants():
    c = np.zeros((P, C_ALL), np.float32)
    p = np.arange(P)
    c[:, C_ID:C_ID + P] = np.eye(P)
    for pos in range(POS):
        c[p, C_SEL + 32 * pos + GO * pos + p // NIB] = 1.0
    c[:, C_KCOL] = p % NIB
    c[:, C_KARR:C_KARR + EXPERTS] = np.arange(1, EXPERTS + 1)
    c[:, C_UP:C_UP + P] = np.where(p[None, :] > p[:, None], MASKED, 0.0)
    c[:, C_LO:C_LO + P] = np.where(p[:, None] > p[None, :], MASKED, 0.0)
    return c


def a_units(causal):
    units = []
    for h in range(QUAD):
        for qt in range(QT):
            n = (qt + 1) * P if causal else SEQ
            for half in range((n + CHUNK - 1) // CHUNK):
                units.append((h, qt, half, n <= CHUNK, half * CHUNK, min(CHUNK, n - half * CHUNK)))
    return units


def b_groups(causal):
    groups = []
    for qh in range(QHS):
        kts = min(QT, (qh + 1) * CHUNK // P) if causal else QT
        for kt in range(kts):
            off = max(0, kt * P - qh * CHUNK) if causal else 0
            groups.append((qh, kt, off, kt == kts - 1))
    return groups


UNITS = [a_units(False), a_units(True)]
GROUPS = [b_groups(False), b_groups(True)]
RING = 3
LAG = 1
LEAD = RING


class Then:
    def __init__(self, eng, sem, base, i, per):
        self.eng, self.sem, self.start, self.n, self.per = eng, sem, per * i + base, 0, per

    def __call__(self, ins, wait=True):
        self.n += 1
        ins.then_inc(self.sem, 1)
        if wait:
            self.eng.wait_ge(self.sem, self.start + self.n)


CHAIN = [40, 20]
WF_LOADS = 12


def program(nc, x, qkvw, bqk0, bv0, ow0, ob0, wbase, bbase, wrout, brout, lora_a, lora_b,
            wq1, wk1, wv1, bqk1, bv1, ow1, ob1, qweight, bd4, bd8, bffn, consts, shifts, out):
    def dram(name, shape, dt=F32):
        return nc.dram_tensor(name, shape, dt).ap()

    qp = [dram(f"q_parts{l}", [PARTS, BATCH * DIM, SEQ], BF16) for l in range(2)]
    kp = [dram(f"k_parts{l}", [PARTS, BATCH * DIM, SEQ], BF16) for l in range(2)]
    vp = [dram(f"v_ones{l}", [STEPS, SEQ, QUAD * VW]) for l in range(2)]
    ctxd = [dram(f"ctx{l}", [BATCH * DIM, SEQ]) for l in range(2)]
    dend = [dram(f"den{l}", [BATCH * HEADS, SEQ]) for l in range(2)]
    rdend = [dram(f"rden{l}", [BATCH * HEADS, SEQ]) for l in range(2)]
    resd = [dram(f"res{l}", [TOK, DIM]) for l in range(2)]
    coded = dram("code_halves", [2, DIM, DIM], BF16)

    with ExitStack() as ctx:
        def sb(name, shape, dt=F32):
            return ctx.enter_context(nc.sbuf_tensor(name, shape, dt))

        def sem(name):
            return ctx.enter_context(nc.semaphore(name))

        def sems(prefix, names):
            return {n: sem(f"{prefix}_{n}") for n in names.split()}

        cst = sb("cst", [P, C_ALL])
        shf = sb("shf", [P, BITS], I32)
        ident = cst[:, C_ID:C_ID + P]
        kcol = cst[:, C_KCOL:C_KCOL + 1]
        karr = cst[:, C_KARR:C_KARR + EXPERTS]
        idb = sb("idb", [P, P], BF16)
        upb = sb("upb", [P, P], BF16)
        lob = sb("lob", [P, P], BF16)
        wqkv = sb("wqkv", [P, KT, 3 * DIM])
        wo = sb("wo", [P, 2, KT, DIM])
        wff = sb("wff", [P, KT, DIM])
        wrl = sb("wrl", [P, KT, EXPERTS * RANK + EXPERTS])
        lb = sb("lb", [P, DIM])
        w4 = sb("w4", [P, KT, DIM])
        w8 = sb("w8", [P, KT, DIM])
        bqk = sb("bqk", [P, 2, QKT])
        bv = sb("bv", [P, 2, DIM])
        rb = sb("rb", [P, 2, DIM])
        brt = sb("brt", [P, EXPERTS])

        ARENA = 24320
        arena = sb("arena", [P, ARENA])

        class Layout:
            def __init__(self):
                self.at = 0

            def take(self, n, dt=F32):
                words = n if dt != BF16 else n // 2
                a = arena[:, self.at:self.at + words]
                self.at += words
                assert self.at <= ARENA, self.at
                return a if dt == F32 else a.bitcast(dt)

        fr = Layout()
        xb = fr.take(TT * DIM).rearrange("p (t d) -> p t d", t=TT)
        xn = fr.take(TT * DIM).rearrange("p (t d) -> p t d", t=TT)
        xr = fr.take(TT * DIM).rearrange("p (t d) -> p t d", t=TT)
        xnt = fr.take(KT * CHUNK).rearrange("p (k t) -> p k t", k=KT)
        cxn = fr.take(KT * CHUNK).rearrange("p (k t) -> p k t", k=KT)
        rdr = fr.take(KT * CHUNK).rearrange("p (k t) -> p k t", k=KT)
        qf = fr.take(2 * CHUNK).rearrange("p (a t) -> p a t", a=2)
        qr = fr.take(2 * CHUNK).rearrange("p (a t) -> p a t", a=2)
        qs = fr.take(2 * PARTS * CHUNK, BF16).rearrange("p (a c t) -> p a c t", a=2, c=PARTS)
        vt = fr.take(2 * HEADS * VW).rearrange("p (a h w) -> p a h w", a=2, h=HEADS)
        hs = fr.take(TT * EXPERTS * RANK).rearrange("p (t e r) -> p t e r", t=TT, e=EXPERTS)
        hw = fr.take(TT * EXPERTS * RANK).rearrange("p (t e r) -> p t e r", t=TT, e=EXPERTS)
        hwt = fr.take(TT * P).rearrange("p (t q) -> p t q", t=TT)
        rt = fr.take(2 * DIM).rearrange("p (a d) -> p a d", a=2)
        ysel = fr.take(2 * DIM).rearrange("p (a d) -> p a d", a=2)
        junk = fr.take(DIM)

        at = Layout()
        qst = at.take(NSTAGE * QUAD * SEQ, BF16).rearrange("p (s h t) -> p s h t", s=NSTAGE, h=QUAD)
        kst = at.take(NSTAGE * QUAD * SEQ, BF16).rearrange("p (s h t) -> p s h t", s=NSTAGE, h=QUAD)
        vst = at.take(NSTAGE * QT * QUAD * VW).rearrange("p (s k w) -> p s k w", s=NSTAGE, k=QT)
        pr = at.take(2 * QUAD * CHUNK).rearrange("p (a h t) -> p a h t", a=2, h=QUAD)

        dq = Layout()
        NB_ = KT * WORDS * BITS
        qwt = dq.take(KT * PLANES * WORDS, I32).rearrange("p (k e w) -> p k e w", k=KT, e=PLANES)
        bits = dq.take(NB_, I32)
        bits2 = dq.take(NB_, I32)
        half = [dq.take(NB_, I32) for _ in range(2)]
        codeb = dq.take(2 * NB_, BF16).rearrange("p (c k i) -> p c k i", c=2, k=KT)
        rep = dq.take(2 * 2 * POS * DIM, BF16).rearrange("p (a c j i) -> p a c j i", a=2, c=2, j=POS)
        oh = dq.take(POS * DIM).rearrange("p (j i) -> p j i", j=POS)
        msk = dq.take(POS * DIM).rearrange("p (j i) -> p j i", j=POS)
        bd8s = dq.take(2 * POS * P).rearrange("p (a j m) -> p a j m", a=2, j=POS)
        bd4s = dq.take(2 * POS * 32).rearrange("p (a j m) -> p a j m", a=2, j=POS)
        wrow = dq.take(2 * DIM).rearrange("p (a i) -> p a i", a=2)

        eps_col = sb("eps_col", [P, 1])
        stats = sb("stats", [P, TT, 6])
        mv = sb("mv", [P, 4, TT])
        std = sb("std", [P, TT])
        rstd = sb("rstd", [P, TT])
        lg = sb("lg", [P, TT, EXPERTS])
        sm = sb("sm", [P, 8, TT, EXPERTS])
        sc = sb("sc", [P, 4, TT])
        nrm = sb("nrm", [P, 4, TT])
        mx = sb("mx", [P, 2, QUAD, QT])
        mmx = sb("mmx", [P, QUAD, QT])
        mrow = sb("mrow", [QUAD * QT, 2, P], BF16)
        cx = sb("cx", [P, 2, CHUNK])
        dn = sb("dn", [P, 2, CHUNK])

        bank = [ctx.enter_context(nc.psum_tensor(f"bank{i}", [P, CHUNK], F32)) for i in range(4)]
        pair = [ctx.enter_context(nc.psum_tensor(f"pair{i}", [P, 2, CHUNK], F32)) for i in range(2)]
        banks = [b[:, :] for b in bank] + [pair[i // 2][:, i % 2, :] for i in range(4)]

        s_cst = sem("s_cst")
        s_wf = sem("s_wf")
        s_w1 = sem("s_w1")
        s_rb = sem("s_rb")
        s_prep = sem("s_prep")
        s_ones = sem("s_ones")
        step = sem("dve_step")
        s_out = sem("s_out")
        D = sems("dq", "qw code code_out0 code_out1 in0 in1 oh tab msk wsum wrow wt wt_used")
        D["in"] = [D["in0"], D["in1"]]
        FRONT = "x_in stat sqrt xn xr tp xnt qk qk_f qk_r qk_3 qk_out0 qk_out1 v v_used v_out0 v_out1 y y_used y_out0 y_out1"
        MIX = " ctx_in ctx_n x1 x_ready"
        F = [sems("f0", FRONT + " h hl_used hw hwt_ps hwt"), sems("f1", FRONT + MIX + " y_sel sq nsqrt mask"),
             sems("f2", "x_in" + MIX)]
        AN = ("a_ready a_used mm mrow mload s_ready e_done pv_done cx cx_out0 cx_out1 den rden rden_out "
              "load0 load1 load2")
        A = [sems(f"a{l}", AN) for l in range(2)]

        block = ctx.enter_context(nc.Block())

        @block.sync
        def _(sp):
            sp.dma_start(cst[:, :], consts).then_inc(s_cst, DMA)
            sp.dma_start(shf[:, :], shifts.partition_broadcast(P)).then_inc(s_cst, DMA)
            sp.dma_start(qwt, qweight.rearrange("(k p) e w -> p k e w", p=P)).then_inc(D["qw"], DMA)

            for c in range(2):
                sp.wait_ge(D["code"], c + 1)
                sp.dma_start(coded[c].rearrange("(k p) i -> p k i", p=P), codeb[:, c]).then_inc(D[f"code_out{c}"], DMA)
            for c in range(2):
                sp.wait_ge(D[f"code_out{c}"], DMA)
            with sp.Fori(0, KT) as ot:
                for pos in range(POS):
                    a = pos % 2
                    if pos >= 2:
                        sp.wait_ge(D["wsum"], POS * ot + pos - 1)
                    else:
                        sp.wait_ge(D["wsum"], POS * ot)
                    for j in range(POS):
                        for c in range(2):
                            rows = coded[c, bass.ds(ot * P + j * 32 + pos * GO, GO), :]
                            sp.dma_start(rep[:, a, c, j, :], rows.unsqueeze(1).to_broadcast([GO, NIB, DIM]))\
                              .then_inc(D["in"][a], DMA)
                    sp.dma_start(bd8s[:, a], bd8[bass.ds(ot * POS + pos, 1)].rearrange("o p j m -> p (o j) m"))\
                      .then_inc(D["in"][a], DMA)
                    sp.dma_start(bd4s[:, a], bd4[bass.ds(ot * POS + pos, 1)].rearrange("o p j m -> p (o j) m"))\
                      .then_inc(D["in"][a], DMA)

            def front_stores(l):
                S = F[l]
                sp.wait_ge(s_ones, 2 * l + 1)
                with sp.Fori(0, BATCH) as b, sp.Fori(0, NCH) as c:
                    i = b * NCH + c
                    for ot in range(QKT):
                        sp.wait_ge(S["qk_3"], QKT * i + ot + 1)
                        parts = (qp if ot < KT else kp)[l]
                        dst = parts[:, bass.ds(b * DIM + ot % KT * P, P), bass.ds(c * CHUNK, CHUNK)]
                        sp.dma_start(dst.rearrange("c p t -> p c t"), qs[:, ot % 2]).then_inc(S[f"qk_out{ot % 2}"], DMA)
                    for t in range(TT):
                        sp.wait_ge(S["v_used"], TT * i + t + 1)
                        dst = vp[l][bass.ds(b * QUADS, QUADS), bass.ds(c * CHUNK + t * P, P), :]
                        sp.dma_start(dst.rearrange("s p w -> p s w"),
                                     vt[:, t % 2].rearrange("p (s h) w -> p s (h w)", s=QUADS))\
                          .then_inc(S[f"v_out{t % 2}"], DMA)
                    for t in range(TT):
                        sp.wait_ge(S["y_used"], TT * i + t + 1)
                        sp.dma_start(resd[l][bass.ds(i * CHUNK + t * P, P), :], rt[:, t % 2])\
                          .then_inc(S[f"y_out{t % 2}"], DMA)
                for n in ("qk_out0", "qk_out1"):
                    sp.wait_ge(S[n], DMA * CHUNKS * QKT // 2)
                for n in ("v_out0", "v_out1", "y_out0", "y_out1"):
                    sp.wait_ge(S[n], DMA * CHUNKS * TT // 2)

            def attention_loads(l):
                S, nb = A[l], len(GROUPS[l])

                def load(it, st):
                    s = S[f"load{st}"]
                    for parts, stage, rows in ((qp[l], qst, Q_ROWS), (kp[l], kst, K_ROWS)):
                        for n, part in enumerate(rows):
                            src = parts[part, bass.ds(it * QUAD * HD, QUAD * HD), :]
                            sp.dma_start(stage[n * HD:(n + 1) * HD, st], src.rearrange("(h d) t -> d h t", d=HD))\
                              .then_inc(s, DMA)
                    src = vp[l][bass.ds(it, 1)].rearrange("o (k p) w -> p (o k) w", p=P)
                    sp.dma_start(vst[:, st], src).then_inc(s, DMA)

                def max_rows(it, st):
                    sp.wait_ge(S["mrow"], it + 1)
                    for n in range(2):
                        r = SROWS + n
                        sp.dma_start(qst[r:r + 1, st].rearrange("o h (q t) -> o (h q) t", t=P), mrow[:, n, :])\
                          .then_inc(S["mload"], DMA)

                for st in range(NSTAGE):
                    load(st, st)
                max_rows(0, 0)
                rounds = (STEPS - 1) // NSTAGE

                def after(it, r, more):
                    max_rows(it + 1, (r + 1) % NSTAGE)
                    if more:
                        sp.wait_ge(S["pv_done"], nb * (it + 1))
                        load(it + NSTAGE, r)

                with sp.Fori(0, rounds - 1) as u:
                    for r in range(NSTAGE):
                        after(u * NSTAGE + r, r, True)
                for it in range(NSTAGE * (rounds - 1), STEPS - 1):
                    after(it, it % NSTAGE, it + NSTAGE < STEPS)
                for n in range(2):
                    sp.wait_ge(S[f"cx_out{n}"], 5 * DMA * STEPS)
                dense = [d[l].rearrange("r (h t) -> (r h) t", t=CHUNK) for d in (dend, rdend)]
                sp.dma_start(dn[:, 0], dense[0]).then_inc(S["den"], DMA)
                sp.wait_ge(S["rden"], 1)
                sp.dma_start(dense[1], dn[:, 1]).then_inc(S["rden_out"], DMA)

            front_stores(0)
            attention_loads(0)
            front_stores(1)
            attention_loads(1)
            with sp.Fori(0, CHUNKS) as i:
                for t in range(TT):
                    sp.wait_ge(F[2]["x_ready"], TT * i + t + 1)
                    sp.dma_start(out[bass.ds(i * CHUNK + t * P, P), :], xb[:, t]).then_inc(s_out, DMA)
            sp.wait_ge(s_out, DMA * TT * CHUNKS)

        @block.gpsimd
        def _(pool):
            w = lambda a: a.rearrange("(k p) n -> p k n", p=P)
            pool.dma_start(wqkv[:, :, :], w(qkvw)).then_inc(s_wf, DMA)
            pool.dma_start(wff[:, :, :], w(wbase)).then_inc(s_wf, DMA)
            pool.dma_start(wrl[:, :, 0:EXPERTS * RANK], w(lora_a)).then_inc(s_wf, DMA)
            pool.dma_start(wrl[:, :, EXPERTS * RANK:], w(wrout)).then_inc(s_wf, DMA)
            pool.dma_start(lb[:, :], lora_b).then_inc(s_wf, DMA)
            for l, (a, b) in enumerate(((bqk0, bv0), (bqk1, bv1))):
                pool.dma_start(bqk[:, l], a).then_inc(s_wf, DMA)
                pool.dma_start(bv[:, l], b.partition_broadcast(P)).then_inc(s_wf, DMA)
            pool.dma_start(brt[:, :], brout.partition_broadcast(P)).then_inc(s_wf, DMA)
            pool.dma_start(wo[:, 0], w(ow0)).then_inc(s_wf, DMA)
            pool.dma_start(wo[:, 1], w(ow1)).then_inc(s_wf, DMA)
            for n, a in enumerate((ob0, bbase, ob1, bffn)):
                pool.dma_start(dn[:, n % 2] if n < 2 else cx[:, n % 2], a.partition_broadcast(P)).then_inc(s_rb, DMA)

            def mix_loads(l, last):
                S, T, pl = F[l], A[l - 1], l - 1
                pool.wait_ge(T["rden_out"], DMA)
                with pool.Fori(0, BATCH) as b, pool.Fori(0, NCH) as c:
                    i = b * NCH + c
                    pool.wait_ge(S["x1"], TT * i)
                    src = ctxd[pl][bass.ds(b * DIM, DIM), bass.ds(c * CHUNK, CHUNK)]
                    pool.dma_start(cxn, src.rearrange("(k p) t -> p k t", p=P)).then_inc(S["ctx_in"], DMA)
                    for k in range(KT):
                        h = P // HD
                        src = rdend[pl][bass.ds(b * HEADS + k * h, h), bass.ds(c * CHUNK, CHUNK)]
                        pool.dma_start(rdr[:, k], src.unsqueeze(1).to_broadcast([h, HD, CHUNK])).then_inc(S["ctx_in"], DMA)
                    if last:
                        pool.wait_ge(s_out, DMA * TT * i)
                    else:
                        pool.wait_ge(S["xn"], TT * i)
                    pool.dma_start(xb, resd[pl][bass.ds(i * CHUNK, CHUNK), :].rearrange("(t p) d -> p t d", p=P))\
                        .then_inc(S["x_in"], DMA)
                    if not last:
                        residual(l, i)

            def residual(l, i):
                S = F[l]
                if l == 0:
                    pool.wait_ge(S["x_in"], DMA * (i + 1))
                else:
                    pool.wait_ge(S["x_ready"], TT * (i + 1))
                pool.wait_ge(S["y_used"], TT * i)
                for t in range(TT):
                    pool.tensor_tensor(xr[:, t], xb[:, t], rb[:, l], ALU.add).then_inc(S["xr"], 1)
                pool.wait_ge(S["xr"], TT * (i + 1))

            pool.wait_ge(D["wt_used"], 2 * KT * KT)
            pool.memset(vt[:, :, :, HD:], 1.0).then_inc(s_ones, 1)
            pool.wait_ge(s_prep, 6)
            with pool.Fori(0, CHUNKS) as i:
                pool.wait_ge(F[0]["xn"], TT * i)
                pool.dma_start(xb, x[bass.ds(i * CHUNK, CHUNK), :].rearrange("(t p) d -> p t d", p=P))\
                    .then_inc(F[0]["x_in"], DMA)
                residual(0, i)

            def context_stores(l):
                S = A[l]

                def store(it, qh):
                    pool.wait_ge(S["cx"], 2 * it + qh + 1)
                    cols = slice(qh * CHUNK, (qh + 1) * CHUNK)
                    for j in range(QUAD):
                        pool.dma_start(ctxd[l][bass.ds(it * QUAD * HD + j * HD, HD), cols],
                                       cx[32 * j:32 * j + HD, qh]).then_inc(S[f"cx_out{qh}"], DMA)
                    pool.dma_start(dend[l][bass.ds(it * QUAD, QUAD), cols], cx[HD:P:32, qh])\
                        .then_inc(S[f"cx_out{qh}"], DMA)

                with pool.Fori(0, STEPS) as it:
                    for qh in range(QHS):
                        store(it, qh)

            def stage_ones(l):
                S = F[l]
                for n in ("qk_out0", "qk_out1"):
                    pool.wait_ge(S[n], DMA * CHUNKS * QKT // 2)
                for n in ("v_out0", "v_out1", "y_out0", "y_out1"):
                    pool.wait_ge(S[n], DMA * CHUNKS * TT // 2)
                pool.memset(kst[SROWS:P], 1.0).then_inc(s_ones, 1)

            stage_ones(0)
            for n, a in enumerate((wq1, wk1, wv1)):
                pool.dma_start(wqkv[:, :, n * DIM:(n + 1) * DIM], w(a)).then_inc(s_w1, DMA)
            context_stores(0)
            pool.wait_ge(A[0]["rden_out"], DMA)
            pool.memset(vt[:, :, :, HD:], 1.0).then_inc(s_ones, 1)
            mix_loads(1, False)
            stage_ones(1)
            context_stores(1)
            mix_loads(2, True)

        @block.scalar
        def _(act):
            copy = lambda o, i: act.activation(o, i, ACT.Copy)
            act.wait_ge(s_cst, 2 * DMA)
            for o, c in ((idb, C_ID), (upb, C_UP), (lob, C_LO)):
                copy(o[:, :], cst[:, c:c + P]).then_inc(s_prep, 1)

            with act.Fori(0, KT) as ot:
                act.wait_ge(D["wsum"], POS * (ot + 1))
                act.wait_ge(D["wt_used"], 2 * KT * ot)
                for n in range(2):
                    copy(wrow[:, n], banks[4 + n]).then_inc(D["wrow"], 1)
                for n in range(2):
                    for k in range(KT):
                        act.wait_ge(D["wt"], 2 * KT * ot + KT * n + k + 1)
                        copy((w4, w8)[n][:, k, bass.ds(ot * P, P)], banks[6 + k % 2][:, 0:P]).then_inc(D["wt_used"], 1)

            act.wait_ge(s_wf, WF_LOADS * DMA)
            act.wait_ge(s_prep, 4)

            def front(l):
                S = F[l]
                with act.Fori(0, CHUNKS) as i:
                    act.wait_ge(S["stat"], (TT + 1) * (i + 1))
                    act.activation(std[:, :], mv[:, 1], ACT.Sqrt, bias=eps_col[:, :]).then_inc(S["sqrt"], 1)
                    if l:
                        for t in range(TT):
                            act.wait_ge(S["xn"], TT * i + t + 1)
                            act.wait_ge(S["sq"], TT * i + t)
                            act.activation(junk, xn[:, t], ACT.Square, accum_out=nrm[:, 0, t:t + 1]).then_inc(S["sq"], 1)
                        act.wait_ge(S["sq"], TT * (i + 1))
                        act.activation(nrm[:, 1], nrm[:, 0], ACT.Sqrt).then_inc(S["nsqrt"], 1)
                    act.wait_ge(S["y"], TT * i)
                    for t in range(TT):
                        act.wait_ge(S["tp"], TT * i + t + 1)
                        copy(xnt[:, :, t * P:(t + 1) * P], banks[t % 2].rearrange("p (k q) -> p k q", k=KT))\
                            .then_inc(S["xnt"], 1)
                    for ot in range(QKT):
                        n = QKT * i + ot
                        act.wait_ge(S["qk"], n + 1)
                        act.wait_ge(S["qk_r"], QKT * i if ot < 2 else n - 1)
                        act.wait_ge(S[f"qk_out{ot % 2}"], DMA * (QKT // 2 * i + ot // 2))
                        src, b = banks[4 + ot % 2], bqk[:, l, ot:ot + 1]
                        act.activation(qf[:, ot % 2], src, ACT.Identity, bias=b).then_inc(S["qk_f"], 1)
                        act.activation(qs[:, ot % 2, 0], src, ACT.Identity, bias=b).then_inc(S["qk_f"], 1)
                    if l == 0:
                        act.wait_ge(S["hwt_ps"], i + 1)
                        copy(hwt, banks[3].rearrange("p (t q) -> p t q", t=TT)).then_inc(S["hwt"], 1)
                    else:
                        for t in range(TT):
                            n = TT * i + t
                            act.wait_ge(S["mask"], 2 * (i + 1))
                            act.wait_ge(S["y"], n + 1)
                            act.wait_ge(S["y_used"], TT * i if t < 2 else n - 1)
                            act.activation(ysel[:, t % 2], banks[6 if t % 2 == 0 else 2], ACT.Copy,
                                           scale=nrm[:, 3, t:t + 1]).then_inc(S["y_sel"], 1)

            def attention(l):
                S, groups = A[l], GROUPS[l]
                nb = len(groups)

                def one(it):
                    first = 0
                    for g, (qh, kt, off, last) in enumerate(groups):
                        for p in range(2):
                            act.wait_ge(S["s_ready"], 2 * nb * it + 2 * g + p + 1)
                            if p == 0:
                                act.wait_ge(S["pv_done"], nb * it + max(0, g - 1))
                            act.activation(pr[:, g % 2, 2 * p:2 * p + 2, off:], pair[p][:, :, off:], ACT.Exp,
                                           scale=SCALE).then_inc(S["e_done"], 1)
                        done = [n for n, q in enumerate(groups) if q[3]]
                        if g == done[0] + 1:
                            evacuate(it, 0, done[0])
                    evacuate(it, 1, done[1])

                def evacuate(it, qh, g):
                    act.wait_ge(S["pv_done"], nb * it + g + 1)
                    act.wait_ge(S[f"cx_out{qh}"], 5 * DMA * it)
                    copy(cx[:, qh], banks[RING]).then_inc(S["cx"], 1)

                with act.Fori(0, STEPS) as it:
                    one(it)

            front(0)
            attention(0)
            front(1)
            attention(1)

        @block.vector
        def _(dve):
            def self_wait(count):
                dve.wait_ge(step, count)

            dve.memset(eps_col[:, :], EPS).then_inc(s_prep, 1)
            dve.wait_ge(s_cst, 2 * DMA)
            dve.wait_ge(D["qw"], DMA)
            n = 0
            shape = [P, KT, WORDS, BITS]
            v = lambda a: a.rearrange("p (k w b) -> p k w b", k=KT, w=WORDS)
            for e in range(PLANES):
                c, s = e // 4, e % 4
                dve.tensor_tensor(v(bits), qwt[:, :, e, :].unsqueeze(3).to_broadcast(shape),
                                  shf[:, :].unsqueeze(1).unsqueeze(1).to_broadcast(shape),
                                  ALU.logical_shift_right).then_inc(step, 1)
                n += 1
                self_wait(n)
                o = half[c] if s == 0 else bits2
                dve.tensor_scalar(o, bits, 1, s, ALU.bitwise_and, ALU.logical_shift_left).then_inc(step, 1)
                n += 1
                self_wait(n)
                if s:
                    dve.tensor_tensor(half[c], half[c], bits2, ALU.bitwise_or).then_inc(step, 1)
                    n += 1
                    self_wait(n)
                if s == 3:
                    dve.tensor_copy(codeb[:, c], half[c].rearrange("p (k i) -> p k i", k=KT)).then_inc(D["code"], 1)
            before = [n]

            with dve.Fori(0, KT) as ot:
                for pos in range(POS):
                    a = pos % 2
                    r = POS * ot + pos
                    dve.wait_ge(D["in"][a], 10 * DMA * (POS // 2 * ot + pos // 2 + 1))
                    dve.wait_ge(D["wsum"], r)
                    for j in range(POS):
                        dve.tensor_scalar(oh[:, j], rep[:, a, 0, j], kcol, None, ALU.is_equal).then_inc(D["oh"], 1)
                    for j in range(POS):
                        dve.wait_ge(D["tab"], POS * r + j + 1)
                        dve.scalar_tensor_tensor(out=msk[:, j], in0=rep[:, a, 1, j], scalar=kcol, in1=banks[j],
                                                 op0=ALU.is_equal, op1=ALU.mult).then_inc(D["msk"], 1)

            dve.wait_ge(s_rb, 4 * DMA)
            dve.wait_ge(s_wf, WF_LOADS * DMA)
            dve.tensor_tensor(rb[:, 0], dn[:, 0], dn[:, 1], ALU.add).then_inc(s_prep, 1)
            dve.tensor_tensor(rb[:, 1], cx[:, 0], cx[:, 1], ALU.add).then_inc(s_prep, 1)

            def mix(l, i):
                S = F[l]
                dve.wait_ge(S["ctx_in"], DMA * (1 + KT) * (i + 1))
                dve.tensor_tensor(cxn, cxn, rdr, ALU.mult).then_inc(S["ctx_n"], 1)
                dve.wait_ge(S["x_in"], DMA * (i + 1))
                for t in range(TT):
                    dve.wait_ge(S["x1"], TT * i + t + 1)
                    dve.tensor_tensor(xb[:, t], banks[2 + t % 2], xb[:, t], ALU.add).then_inc(S["x_ready"], 1)

            def sparsemax(then):
                srt, cum, kz, sup, sel, w = (sm[:, n] for n in range(6))
                k4 = karr.unsqueeze(1).to_broadcast([P, TT, EXPERTS])
                for t in range(TT):
                    then(dve.max(srt[:, t], lg[:, t]), wait=t == TT - 1)
                then(dve.tensor_copy(cum[:, :, 0:1], srt[:, :, 0:1]))
                for e in range(1, EXPERTS):
                    then(dve.tensor_tensor(cum[:, :, e:e + 1], cum[:, :, e - 1:e], srt[:, :, e:e + 1], ALU.add))
                then(dve.tensor_tensor(kz, srt, k4, ALU.mult))
                then(dve.tensor_scalar(kz, kz, 1.0, None, ALU.add))
                then(dve.tensor_tensor(sup, kz, cum, ALU.is_gt))
                then(dve.reduce_sum(sc[:, 0], sup, AX))
                kb = sc[:, 0].unsqueeze(2).to_broadcast([P, TT, EXPERTS])
                then(dve.tensor_tensor(sel, k4, kb, ALU.is_equal))
                then(dve.tensor_tensor(sel, sel, cum, ALU.mult))
                then(dve.reduce_sum(sc[:, 1], sel, AX))
                then(dve.tensor_scalar(sc[:, 1], sc[:, 1], -1.0, None, ALU.add))
                then(dve.reciprocal(sc[:, 2], sc[:, 0]))
                then(dve.tensor_tensor(sc[:, 3], sc[:, 1], sc[:, 2], ALU.mult))
                tb = sc[:, 3].unsqueeze(2).to_broadcast([P, TT, EXPERTS])
                then(dve.tensor_tensor(w, lg[:, :, :], tb, ALU.subtract))
                then(dve.tensor_scalar(w, w, 0.0, None, ALU.max))
                return w

            def front(l):
                S = F[l]
                per = CHAIN[l]
                base = before[0]
                with dve.Fori(0, CHUNKS) as i:
                    then = Then(dve, step, base, i, per)
                    if l:
                        mix(l, i)
                        dve.wait_ge(S["x_ready"], TT * (i + 1))
                    else:
                        dve.wait_ge(S["x_in"], DMA * (i + 1))
                    for t in range(TT):
                        dve.bn_stats(stats[:, t], xb[:, t]).then_inc(S["stat"], 1)
                    dve.wait_ge(S["stat"], (TT + 1) * i + TT)
                    (em, es), (om, os_) = ((stats[:, :, n], stats[:, :, n + 1]) for n in (1, 4))
                    mean, var, dif, dev = (mv[:, n] for n in range(4))
                    then(dve.tensor_tensor(mean, em, om, ALU.add), wait=False)
                    then(dve.tensor_tensor(dif, em, om, ALU.subtract), wait=False)
                    then(dve.tensor_tensor(dev, es, os_, ALU.add))
                    then(dve.tensor_scalar(mean, mean, 0.5, None, ALU.mult), wait=False)
                    then(dve.tensor_tensor(dif, dif, dif, ALU.mult))
                    then(dve.tensor_scalar(dif, dif, 0.25, None, ALU.mult), wait=False)
                    then(dve.tensor_scalar(dev, dev, 1.0 / DIM, None, ALU.mult))
                    dve.tensor_tensor(var, dif, dev, ALU.add).then_inc(S["stat"], 1)
                    dve.wait_ge(S["sqrt"], i + 1)
                    then(dve.reciprocal(rstd[:, :], std[:, :]))
                    for t in range(TT):
                        if t == 0:
                            dve.wait_ge(S["tp"], TT * i)
                        dve.tensor_scalar(xn[:, t], xb[:, t], mv[:, 0, t:t + 1], rstd[:, t:t + 1], ALU.subtract, ALU.mult)\
                           .then_inc(S["xn"], 1)
                    if l == 0:
                        dve.wait_ge(S["h"], 2 * i + 2)
                        dve.tensor_tensor(lg[:, :, :], banks[3][:, 0:TT * EXPERTS].rearrange("p (t e) -> p t e", t=TT),
                                          brt[:, :].unsqueeze(1).to_broadcast([P, TT, EXPERTS]), ALU.add)\
                           .then_inc(S["hl_used"], 1)
                        dve.wait_ge(S["hl_used"], 2 * i + 1)
                        dve.tensor_copy(hs.rearrange("p t e r -> p (t e r)"), banks[2]).then_inc(S["hl_used"], 1)
                        w = sparsemax(then)
                        for t in range(TT):
                            dve.tensor_tensor(hw[:, t], hs[:, t], w[:, t].unsqueeze(2).to_broadcast([P, EXPERTS, RANK]),
                                              ALU.mult).then_inc(S["hw"], 1)
                    else:
                        dve.wait_ge(S["nsqrt"], i + 1)
                        dve.tensor_scalar(nrm[:, 2], nrm[:, 1], NORM_T, None, ALU.is_gt).then_inc(S["mask"], 1)
                        dve.tensor_scalar(nrm[:, 3], nrm[:, 1], NORM_T, None, ALU.is_le).then_inc(S["mask"], 1)
                    for ot in range(QKT):
                        n = QKT * i + ot
                        a = ot % 2
                        dve.wait_ge(S["qk_f"], 2 * (n + 1))
                        dve.tensor_tensor(qr[:, a], qf[:, a], qs[:, a, 0], ALU.subtract).then_inc(S["qk_r"], 1)
                        dve.wait_ge(S["qk_r"], n + 1)
                        then(dve.tensor_copy(qs[:, a, 1], qr[:, a]))
                        dve.tensor_tensor(qs[:, a, 2], qr[:, a], qs[:, a, 1], ALU.subtract).then_inc(S["qk_3"], 1)
                    for t in range(TT):
                        n = TT * i + t
                        dve.wait_ge(S["v"], n + 1)
                        dve.wait_ge(S[f"v_out{t % 2}"], DMA * (TT // 2 * i + t // 2))
                        h3 = lambda a: a.rearrange("p (h d) -> p h d", h=HEADS)
                        dve.tensor_tensor(vt[:, t % 2, :, 0:HD], h3(banks[6 + t % 2]), h3(bv[:, l]), ALU.add)\
                           .then_inc(S["v_used"], 1)
                    dve.wait_ge(S["xr"], TT * (i + 1))
                    for t in range(TT):
                        n = TT * i + t
                        dve.wait_ge(S["y"], n + 1)
                        dve.wait_ge(S[f"y_out{t % 2}"], DMA * (TT // 2 * i + t // 2))
                        if l == 0:
                            dve.tensor_tensor(rt[:, t % 2], banks[6 + t % 2], xr[:, t], ALU.add).then_inc(S["y_used"], 1)
                        else:
                            dve.wait_ge(S["y_sel"], n + 1)
                            then(dve.scalar_tensor_tensor(out=ysel[:, t % 2], in0=banks[7 if t % 2 == 0 else 3],
                                                          scalar=nrm[:, 2, t:t + 1], in1=ysel[:, t % 2],
                                                          op0=ALU.mult, op1=ALU.add))
                            dve.tensor_tensor(rt[:, t % 2], ysel[:, t % 2], xr[:, t], ALU.add).then_inc(S["y_used"], 1)
                    assert then.n == per, then.n
                before[0] = base + per * CHUNKS

            def attention(l):
                S, units = A[l], UNITS[l]
                na = len(units)
                base = before[0]

                def maxima(it):
                    for k, (h, qt, hf, only, k0, n) in enumerate(units):
                        dve.wait_ge(S["a_ready"], (na + 1) * it + k + 1)
                        o = mmx[:, h, qt:qt + 1] if only else mx[:, hf, h, qt:qt + 1]
                        dve.reduce_max(o, banks[k % RING][:, 0:n], AX).then_inc(S["a_used"], 1)
                    dve.wait_ge(S["a_used"], na * (it + 1))
                    q0 = min(qt for _, qt, _, only, _, _ in units if not only)
                    dve.tensor_tensor(mmx[:, :, q0:], mx[:, 0, :, q0:], mx[:, 1, :, q0:], ALU.max).then_inc(S["mm"], 1)
                    dve.wait_ge(S["a_ready"], (na + 1) * (it + 1))
                    dve.wait_ge(S["mload"], 2 * DMA * it)
                    rows = banks[na % RING][0:QUAD * QT, 0:P]
                    dve.tensor_scalar(mrow[:, 0], rows, -1.0, None, ALU.mult).then_inc(step, 1)
                    dve.wait_ge(step, base + it + 1)
                    dve.scalar_tensor_tensor(out=mrow[:, 1], in0=rows, scalar=-1.0, in1=mrow[:, 0],
                                             op0=ALU.mult, op1=ALU.subtract).then_inc(S["mrow"], 1)

                with dve.Fori(0, STEPS) as it:
                    maxima(it)
                before[0] = base + STEPS
                dve.wait_ge(S["den"], DMA)
                dve.reciprocal(dn[:, 1], dn[:, 0]).then_inc(S["rden"], 1)

            front(0)
            attention(0)
            front(1)
            attention(1)
            with dve.Fori(0, CHUNKS) as i:
                mix(2, i)

        @block.tensor
        def _(pe):
            def product(o, pairs, start=True, stop=True):
                for n, (a, b) in enumerate(pairs):
                    last = pe.matmul(o, a, b, start=start and n == 0, stop=stop and n == len(pairs) - 1)
                return last

            pe.wait_ge(s_cst, 2 * DMA)
            with pe.Fori(0, KT) as ot:
                for pos in range(POS):
                    a, r = pos % 2, POS * ot + pos
                    pe.wait_ge(D["in"][a], 10 * DMA * (POS // 2 * ot + pos // 2 + 1))
                    pe.wait_ge(D["msk"], POS * r)
                    for j in range(POS):
                        pe.wait_ge(D["oh"], POS * r + j + 1)
                        product(banks[j], [(bd8s[:, a, j], oh[:, j])]).then_inc(D["tab"], 1)
                    pe.wait_ge(D["wrow"], 2 * ot)
                    for j in range(POS):
                        product(banks[4][32 * j:32 * j + 32], [(bd4s[:, a, j], oh[:, j])],
                                start=pos == 0, stop=pos == POS - 1)
                    for j in range(POS):
                        pe.wait_ge(D["msk"], POS * r + j + 1)
                        last = product(banks[5][32 * j:32 * j + 32],
                                       [(cst[:, C_SEL + 32 * pos:C_SEL + 32 * pos + 32], msk[:, j])],
                                       start=pos == 0, stop=pos == POS - 1)
                    last.then_inc(D["wsum"], 1)
                for n in range(2):
                    pe.wait_ge(D["wrow"], 2 * ot + n + 1)
                    for k in range(KT):
                        m = KT * n + k
                        pe.wait_ge(D["wt_used"], 2 * KT * ot + (m - 1 if m >= 2 else 0))
                        pe.transpose(banks[6 + k % 2][:, 0:P], wrow[:, n, k * P:(k + 1) * P], ident)\
                          .then_inc(D["wt"], 1)

            def project(l, i):
                S = F[l]
                pe.wait_ge(S["ctx_n"], i + 1)
                for t in range(TT):
                    n = TT * i + t
                    if t >= 2:
                        pe.wait_ge(S["x_ready"], n - 1)
                    else:
                        pe.wait_ge(S["y_used"] if l == 1 else S["x_ready"], TT * i)
                    product(banks[2 + t % 2], [(cxn[:, k, t * P:(t + 1) * P], wo[:, l - 1, k]) for k in range(KT)])\
                        .then_inc(S["x1"], 1)

            def front(l):
                S = F[l]
                ER = EXPERTS * RANK
                with pe.Fori(0, CHUNKS) as i:
                    if l:
                        project(l, i)
                    for t in range(TT):
                        n = TT * i + t
                        pe.wait_ge(S["xn"], n + 1)
                        pe.wait_ge(S["xnt"], n - 1 if t >= 2 else TT * i)
                        for k in range(KT):
                            last = pe.transpose(banks[t % 2][:, k * P:(k + 1) * P], xn[:, t, k * P:(k + 1) * P], ident)
                        last.then_inc(S["tp"], 1)
                    pe.wait_ge(S["xnt"], TT * (i + 1))
                    tok = lambda k, t: xnt[:, k, t * P:(t + 1) * P]
                    if l == 0:
                        pe.wait_ge(S["hl_used"], 2 * i)
                        for t in range(TT):
                            last = product(banks[2][:, t * ER:(t + 1) * ER],
                                           [(tok(k, t), wrl[:, k, 0:ER]) for k in range(KT)])
                        last.then_inc(S["h"], 1)
                        pe.wait_ge(S["hwt"], i)
                        for t in range(TT):
                            last = product(banks[3][:, t * EXPERTS:(t + 1) * EXPERTS],
                                           [(tok(k, t), wrl[:, k, ER:]) for k in range(KT)])
                        last.then_inc(S["h"], 1)
                    for ot in range(QKT):
                        n = QKT * i + ot
                        pe.wait_ge(S["qk_f"], 2 * (n - 1) if ot >= 2 else 2 * QKT * i)
                        product(banks[4 + ot % 2], [(wqkv[:, k, ot * P:(ot + 1) * P], xnt[:, k]) for k in range(KT)])\
                            .then_inc(S["qk"], 1)
                    if l == 0:
                        pe.wait_ge(S["hw"], TT * (i + 1))
                        for t in range(TT):
                            last = pe.transpose(banks[3][:, t * P:(t + 1) * P], hw[:, t].rearrange("p e r -> p (e r)"), ident)
                        last.then_inc(S["hwt_ps"], 1)
                    for t in range(TT):
                        n = TT * i + t
                        if t >= 2:
                            pe.wait_ge(S["v_used"], n - 1)
                        else:
                            pe.wait_ge(S["y_used"], TT * i)
                        product(banks[6 + t % 2], [(tok(k, t), wqkv[:, k, 2 * DIM:]) for k in range(KT)])\
                            .then_inc(S["v"], 1)
                    if l == 0:
                        pe.wait_ge(S["hwt"], i + 1)
                    for t in range(TT):
                        n = TT * i + t
                        if t >= 2:
                            pe.wait_ge(S["y_used"], n - 1)
                        else:
                            pe.wait_ge(S["v_used"], TT * i + (TT if l else t + 3))
                        if l == 0:
                            product(banks[6 + t % 2], [(tok(k, t), wff[:, k]) for k in range(KT)] + [(hwt[:, t], lb[:, :])])\
                                .then_inc(S["y"], 1)
                        else:
                            lo, hi = (6, 7) if t % 2 == 0 else (2, 3)
                            product(banks[lo], [(tok(k, t), w4[:, k]) for k in range(KT)])
                            product(banks[hi], [(tok(k, t), w8[:, k]) for k in range(KT)]).then_inc(S["y"], 1)

            def attention(l):
                S, units, groups = A[l], UNITS[l], GROUPS[l]
                na, nb, causal = len(units), len(groups), l == 1

                def score_tile(it, st, k):
                    h, qt, _, _, k0, n = units[k]
                    if k < RING:
                        pe.wait_ge(S["a_used"], na * it)
                        pe.wait_ge(S["mrow"], it)
                    else:
                        pe.wait_ge(S["a_used"], na * it + k - RING + 1)
                    diagonal = causal and k0 + n == (qt + 1) * P
                    ins = pe.matmul(banks[k % RING][:, 0:n], qst[0:SROWS, st, h, qt * P:(qt + 1) * P],
                                    kst[0:SROWS, st, h, k0:k0 + n], start=True, stop=not diagonal)
                    if diagonal:
                        ins = pe.matmul(banks[k % RING][:, n - P:n], idb[:, :], upb[:, :], start=False, stop=True)
                    ins.then_inc(S["a_ready"], 1)

                def maxima_rows(it):
                    pe.wait_ge(S["mm"], it + 1)
                    pe.transpose(banks[na % RING][0:QUAD * QT, 0:P], mmx[:, :, :].rearrange("p h q -> p (h q)"), ident)\
                        .then_inc(S["a_ready"], 1)

                def transposed_scores(it, st, g, p):
                    qh, kt, off, _ = groups[g]
                    pe.wait_ge(S["e_done"], 2 * nb * it + (2 * g + p - 1 if g else 0))
                    diagonal = causal and kt * P >= qh * CHUNK
                    for n in range(2):
                        h = 2 * p + n
                        ins = pe.matmul(pair[p][:, n, off:], kst[0:BROWS, st, h, kt * P:(kt + 1) * P],
                                        qst[0:BROWS, st, h, qh * CHUNK + off:(qh + 1) * CHUNK],
                                        start=True, stop=not diagonal)
                        if diagonal:
                            ins = pe.matmul(pair[p][:, n, off:off + P], idb[:, :], lob[:, :], start=False, stop=True)
                    ins.then_inc(S["s_ready"], 1)

                def weigh_values(it, st, g):
                    qh, kt, off, last = groups[g]
                    pe.wait_ge(S["e_done"], 2 * nb * it + 2 * g + 2)
                    if kt == 0:
                        pe.wait_ge(S["cx"], 2 * it + qh)
                    for j in range(QUAD):
                        ins = pe.matmul(banks[RING][VW * j:VW * (j + 1), off:], vst[:, st, kt, VW * j:VW * (j + 1)],
                                        pr[:, g % 2, j, off:], start=kt == 0, stop=last)
                    ins.then_inc(S["pv_done"], 1)

                def step_(it, st, nxt):
                    tiles = iter(range(na if nxt else 0))

                    def ahead(n):
                        for _, k in list(zip(range(n), tiles)):
                            score_tile(ait, ast, k)
                            if k == na - 1:
                                left.append(LAG)

                    left = []
                    if nxt:
                        ait, ast, loads = nxt
                        pe.wait_ge(S[f"load{ast}"], LOADS * DMA * loads)
                        ahead(LEAD)
                    pe.wait_ge(S["mload"], 2 * DMA * (it + 1))
                    for g in range(nb):
                        transposed_scores(it, st, g, 0)
                        ahead(1)
                        transposed_scores(it, st, g, 1)
                        ahead(2 if g % 4 == 0 else 1)
                        if left and left[0] == 0:
                            maxima_rows(ait)
                        left = [n - 1 for n in left]
                        if g:
                            weigh_values(it, st, g - 1)
                        ahead(2)
                    assert not nxt or left[0] < 0
                    weigh_values(it, st, nb - 1)

                pe.wait_ge(F[l]["y_used"], TT * CHUNKS)
                pe.wait_ge(s_ones, 2 * l + 2)
                pe.wait_ge(S["load0"], LOADS * DMA)
                for k in range(na):
                    score_tile(0, 0, k)
                maxima_rows(0)
                with pe.Fori(0, (STEPS - 1) // NSTAGE) as u:
                    for r in range(NSTAGE):
                        it = u * NSTAGE + r
                        step_(it, r, (it + 1, (r + 1) % NSTAGE, u + 1 + (r + 1) // NSTAGE))
                step_(STEPS - 1, (STEPS - 1) % NSTAGE, None)

            pe.wait_ge(s_wf, WF_LOADS * DMA)
            pe.wait_ge(s_prep, 4)
            front(0)
            attention(0)
            pe.wait_ge(s_w1, 3 * DMA)
            pe.wait_ge(D["wt_used"], 2 * KT * KT)
            pe.wait_ge(A[0]["cx"], 2 * STEPS)
            front(1)
            attention(1)
            pe.wait_ge(A[1]["cx"], 2 * STEPS)
            with pe.Fori(0, CHUNKS) as i:
                project(2, i)


def kernel(**inputs):
    import concourse.bacc as _bacc
    from concourse.bass_utils import run_bass_kernel_spmd as _run

    g = {k: np.asarray(v) for k, v in inputs.items()}
    c = np.ascontiguousarray
    lut4 = g["L1_ffn_lut4"].reshape(KT, 4, POS, GO, NIB).transpose(0, 2, 3, 1, 4)
    lut8 = g["L1_ffn_lut8"].reshape(KT, 4, POS, GO, NIB, NIB).transpose(0, 2, 3, 1, 4, 5)
    bd4 = np.zeros((KT, POS, GO, NIB, 4, POS, GO), np.float32)
    bd8 = np.zeros((KT, POS, GO, NIB, 4, GO, NIB), np.float32)
    for f in range(GO):
        bd8[:, :, f, :, :, f, :] = lut8[:, :, f].transpose(0, 1, 4, 2, 3)
        for pos in range(POS):
            bd4[:, pos, f, :, :, pos, f] = lut4[:, pos, f].transpose(0, 2, 1)
    tiles = lambda b: c(b[:2 * DIM].reshape(QKT, P).T)
    bqk1 = np.concatenate([g["L1_attn_bq"], g["L1_attn_bk"]])
    arrays = {
        "x": g["L0_attn_x"].reshape(TOK, DIM),
        "qkvw": g["L0_attn_attn_qkvw"],
        "bqk0": tiles(g["L0_attn_attn_qkvb"]),
        "bv0": c(g["L0_attn_attn_qkvb"][2 * DIM:]),
        "ow0": g["L0_attn_attn_ow"],
        "ob0": g["L0_attn_attn_ob"],
        "wbase": c(g["L0_ffn_W_base"].T),
        "bbase": g["L0_ffn_b_base"],
        "wrout": c(g["L0_ffn_W_router"].T),
        "brout": g["L0_ffn_b_router"],
        "lora_a": c(g["L0_ffn_lora_A"].transpose(1, 0, 2).reshape(DIM, EXPERTS * RANK)),
        "lora_b": g["L0_ffn_lora_B"].reshape(EXPERTS * RANK, DIM),
        "wq1": c(g["L1_attn_Wq"].T),
        "wk1": c(g["L1_attn_Wk"].T),
        "wv1": c(g["L1_attn_Wv"].T),
        "bqk1": tiles(bqk1),
        "bv1": g["L1_attn_bv"],
        "ow1": c(g["L1_attn_Wo"].T),
        "ob1": g["L1_attn_bo"],
        "qweight": c(g["L1_ffn_qweight"].transpose(1, 0, 2)),
        "bd4": bd4.reshape(KT * POS, P, 4, 32),
        "bd8": bd8.reshape(KT * POS, P, 4, P),
        "bffn": g["L1_ffn_bias"],
        "consts": constants(),
        "shifts": np.arange(BITS, dtype=np.int32),
    }
    nc = _bacc.Bacc("TRN2", target_bir_lowering=False, num_devices=1)
    args = [nc.dram_tensor(f"in_{n}", a.shape, mybir.dt.from_np(a.dtype), kind="ExternalInput").ap()
            for n, a in arrays.items()]
    args.append(nc.dram_tensor("out_0", (TOK, DIM), F32, kind="ExternalOutput").ap())
    program(nc, *args)
    r = _run(nc, [{f"in_{n}": c(a) for n, a in arrays.items()}], core_ids=[0])
    return r.results[0]["out_0"].reshape(BATCH, SEQ, DIM)
```

```python
from contextlib import ExitStack

import numpy as np

import concourse.bass as bass
from concourse import mybir

F32 = mybir.dt.float32
BF16 = mybir.dt.bfloat16
I32 = mybir.dt.int32
ALU = mybir.AluOpType
ACT = mybir.ActivationFunctionType
AX = mybir.AxisListType.X

P = 128
BATCH, SEQ, DIM = 2, 1024, 512
HEADS, HD = 32, 16
TOK = BATCH * SEQ
KT = DIM // P
CHUNK = 512
TT = CHUNK // P
NCH = SEQ // CHUNK
CHUNKS = BATCH * NCH
QUAD = 4
QUADS = HEADS // QUAD
STEPS = BATCH * QUADS
VW = 2 * HD
PARTS = 3
Q_ROWS = (0, 0, 0, 1, 1, 2)
K_ROWS = (0, 1, 2, 0, 1, 0)
SROWS = len(Q_ROWS) * HD
BROWS = SROWS + 2
QT = SEQ // P
QHS = SEQ // CHUNK
EXPERTS, RANK = 8, 16
NSTAGE = 3
QKT = 2 * DIM // P
PLANES, WORDS, BITS = 8, 16, 32
GO = 8
NIB = 16
POS = 4
LOADS = len(Q_ROWS) + len(K_ROWS) + 1
DMA = 16
EPS = 1e-5
SCALE = 1.0 / float(np.sqrt(HD))
MASKED = -1e38
NORM_T = 64.0

C_ID = 0
C_SEL = C_ID + P
C_KCOL = C_SEL + POS * 32
C_KARR = C_KCOL + 1
C_UP = C_KARR + EXPERTS
C_LO = C_UP + P
C_ALL = C_LO + P


def constants():
    c = np.zeros((P, C_ALL), np.float32)
    p = np.arange(P)
    c[:, C_ID:C_ID + P] = np.eye(P)
    for pos in range(POS):
        c[p, C_SEL + 32 * pos + GO * pos + p // NIB] = 1.0
    c[:, C_KCOL] = p % NIB
    c[:, C_KARR:C_KARR + EXPERTS] = np.arange(1, EXPERTS + 1)
    c[:, C_UP:C_UP + P] = np.where(p[None, :] > p[:, None], MASKED, 0.0)
    c[:, C_LO:C_LO + P] = np.where(p[:, None] > p[None, :], MASKED, 0.0)
    return c


def a_units(causal):
    units = []
    for h in range(QUAD):
        for qt in range(QT):
            n = (qt + 1) * P if causal else SEQ
            for half in range((n + CHUNK - 1) // CHUNK):
                units.append((h, qt, half, n <= CHUNK, half * CHUNK, min(CHUNK, n - half * CHUNK)))
    return units


def b_groups(causal):
    groups = []
    for qh in range(QHS):
        kts = min(QT, (qh + 1) * CHUNK // P) if causal else QT
        for kt in range(kts):
            off = max(0, kt * P - qh * CHUNK) if causal else 0
            groups.append((qh, kt, off, kt == kts - 1))
    return groups


UNITS = [a_units(False), a_units(True)]
GROUPS = [b_groups(False), b_groups(True)]
RING = 3
LAG = 1
LEAD = RING


class Then:
    def __init__(self, eng, sem, base, i, per):
        self.eng, self.sem, self.start, self.n, self.per = eng, sem, per * i + base, 0, per

    def __call__(self, ins, wait=True):
        self.n += 1
        ins.then_inc(self.sem, 1)
        if wait:
            self.eng.wait_ge(self.sem, self.start + self.n)


CHAIN = [62, 20]
ONE = 1
PROJECT = 2
LN_STATS = 4


def program(nc, x, qkvw, bqk0, bv0, ow0, ob0, wbase, bbase, wrout, brout, lora_a, lora_b,
            wq1, wk1, wv1, bqk1, bv1, ow1, ob1, qweight, bd4, bd8, bffn, consts, shifts, out):
    def dram(name, shape, dt=F32):
        return nc.dram_tensor(name, shape, dt).ap()

    qp = [dram(f"q_parts{l}", [PARTS, BATCH * DIM, SEQ], BF16) for l in range(2)]
    kp = [dram(f"k_parts{l}", [PARTS, BATCH * DIM, SEQ], BF16) for l in range(2)]
    vp = [dram(f"v_ones{l}", [STEPS, SEQ, QUAD * VW]) for l in range(2)]
    ctxd = [dram(f"ctx{l}", [BATCH * DIM, SEQ]) for l in range(2)]
    dend = [dram(f"den{l}", [BATCH * HEADS, SEQ]) for l in range(2)]
    rdend = [dram(f"rden{l}", [BATCH * HEADS, SEQ]) for l in range(2)]
    resd = [dram(f"res{l}", [TOK, DIM]) for l in range(2)]
    coded = dram("code_halves", [KT, POS, GO, 4, 2, DIM], BF16)

    with ExitStack() as ctx:
        def sb(name, shape, dt=F32):
            return ctx.enter_context(nc.sbuf_tensor(name, shape, dt))

        def sem(name):
            return ctx.enter_context(nc.semaphore(name))

        def sems(prefix, names):
            return {n: sem(f"{prefix}_{n}") for n in names.split()}

        cst = sb("cst", [P, C_ALL])
        shf = sb("shf", [P, BITS], I32)
        ident = cst[:, C_ID:C_ID + P]
        kcol = cst[:, C_KCOL:C_KCOL + 1]
        karr = cst[:, C_KARR:C_KARR + EXPERTS]
        idb = sb("idb", [P, P], BF16)
        upb = sb("upb", [P, P], BF16)
        lob = sb("lob", [P, P], BF16)
        wqkv = sb("wqkv", [P, KT, 3 * DIM])
        wo = sb("wo", [P, 2, KT, DIM])
        wrl = sb("wrl", [P, KT, EXPERTS * RANK + EXPERTS])
        lb = sb("lb", [P, DIM])
        w4 = sb("w4", [P, KT, DIM])
        w8 = sb("w8", [P, KT, DIM])
        wff = w4
        bqk = sb("bqk", [P, 2, QKT])
        bv = sb("bv", [P, 2, DIM])
        rb = sb("rb", [P, 2, DIM])
        rbp = sb("rbp", [P, 2, 2, DIM])
        brt = sb("brt", [P, EXPERTS])
        qwt = sb("qwt", [P, KT, PLANES, WORDS], I32)

        STAGE = QUAD * SEQ + QT * QUAD * VW
        FRONT_WORDS = 20480
        arena = sb("arena", [P, FRONT_WORDS + STAGE])

        class Layout:
            def __init__(self, at, end=FRONT_WORDS):
                self.at, self.end = at, end

            def take(self, n, dt=F32):
                words = n if dt != BF16 else n // 2
                a = arena[:, self.at:self.at + words]
                self.at += words
                assert self.at <= self.end, self.at
                return a if dt == F32 else a.bitcast(dt)

        def stage(at):
            a = Layout(at, FRONT_WORDS + STAGE)
            q, k = (a.take(QUAD * SEQ, BF16).rearrange("p (h t) -> p h t", h=QUAD) for _ in range(2))
            return q, k, a.take(QT * QUAD * VW).rearrange("p (k w) -> p k w", k=QT)

        qst, kst, vst = zip(stage(FRONT_WORDS), stage(0), stage(STAGE))
        pr = Layout(2 * STAGE).take(2 * QUAD * CHUNK).rearrange("p (a h t) -> p a h t", a=2, h=QUAD)

        fr = Layout(0)
        cxn = fr.take(KT * CHUNK).rearrange("p (k t) -> p k t", k=KT)
        rdr = fr.take(KT * CHUNK).rearrange("p (k t) -> p k t", k=KT)
        xb = fr.take(TT * DIM).rearrange("p (t d) -> p t d", t=TT)
        assert fr.at <= 2 * STAGE
        xn = fr.take(TT * DIM).rearrange("p (t d) -> p t d", t=TT)
        xr = fr.take(TT * DIM).rearrange("p (t d) -> p t d", t=TT)
        xnt = fr.take(KT * CHUNK).rearrange("p (k t) -> p k t", k=KT)
        qf = fr.take(2 * CHUNK).rearrange("p (a t) -> p a t", a=2)
        qr = fr.take(2 * CHUNK).rearrange("p (a t) -> p a t", a=2)
        qs = fr.take(2 * PARTS * CHUNK, BF16).rearrange("p (a c t) -> p a c t", a=2, c=PARTS)
        vt = fr.take(2 * HEADS * VW).rearrange("p (a h w) -> p a h w", a=2, h=HEADS)
        rt = fr.take(2 * DIM).rearrange("p (a d) -> p a d", a=2)
        f0 = Layout(0, 2 * KT * CHUNK)
        bits, bits2, half0, half1 = (f0.take(WORDS * BITS, I32).bitcast(I32) for _ in range(4))
        half = (half0, half1)
        codeb = f0.take(2 * DIM, BF16).rearrange("p (c i) -> p c i", c=2)
        f0 = Layout(fr.at)
        hs, hw = (f0.take(TT * EXPERTS * RANK).rearrange("p (t e r) -> p t e r", t=TT, e=EXPERTS) for _ in range(2))
        hwt = f0.take(TT * P).rearrange("p (t q) -> p t q", t=TT)
        f1 = Layout(fr.at)
        ysel = f1.take(2 * DIM).rearrange("p (a d) -> p a d", a=2)
        junk = f1.take(DIM)

        dq = Layout(STAGE)
        rep = dq.take(2 * 2 * POS * DIM, BF16).rearrange("p (a j c i) -> p a j c i", a=2, c=2, j=POS)
        oh = dq.take(2 * POS * DIM).rearrange("p (a j i) -> p a j i", a=2, j=POS)
        msk = dq.take(2 * POS * DIM).rearrange("p (a j i) -> p a j i", a=2, j=POS)
        bd8s = dq.take(2 * POS * P).rearrange("p (a j m) -> p a j m", a=2, j=POS)
        bd4s = dq.take(2 * POS * 32).rearrange("p (a j m) -> p a j m", a=2, j=POS)
        wrow = dq.take(2 * DIM).rearrange("p (a i) -> p a i", a=2)

        eps_col = sb("eps_col", [P, 1])
        stats = sb("stats", [P, TT, 6])
        mv = sb("mv", [P, 4, TT])
        std = sb("std", [P, TT])
        rstd = sb("rstd", [P, TT])
        lg = sb("lg", [P, TT, EXPERTS])
        sm = sb("sm", [P, 8, TT, EXPERTS])
        sc = sb("sc", [P, 4, TT])
        nrm = sb("nrm", [P, 4, TT])
        mx = sb("mx", [P, 2, QUAD, QT])
        mmx = sb("mmx", [P, QUAD, QT])
        mrow = sb("mrow", [QUAD * QT, 2, P], BF16)
        cx = sb("cx", [P, 2, CHUNK])
        DW = QUAD * SEQ // P
        dni = sb("dni", [P, DW])
        dno = sb("dno", [P, DW])

        bank = [ctx.enter_context(nc.psum_tensor(f"bank{i}", [P, CHUNK], F32)) for i in range(4)]
        pair = [ctx.enter_context(nc.psum_tensor(f"pair{i}", [P, 2, CHUNK], F32)) for i in range(2)]
        banks = [b[:, :] for b in bank] + [pair[i // 2][:, i % 2, :] for i in range(4)]

        s_cst = sem("s_cst")
        s_wrl = sem("s_wrl")
        s_wqk = sem("s_wqk")
        s_wv = sem("s_wv")
        s_wy = sem("s_wy")
        s_wo = sem("s_wo")
        s_w1 = sem("s_w1")
        s_rb = sem("s_rb")
        s_prep = sem("s_prep")
        s_ones = sem("s_ones")
        step = sem("dve_step")
        D = sems("dq", "qw code code_out in0 in1 oh tab wl msk wsum wrow wt wt_used")
        D["in"] = [D["in0"], D["in1"]]
        FRONT = "x_in stat sqrt xn xr tp xnt qk qk_f qk_r qk_3 qk_out0 qk_out1 v v_used v_out0 v_out1 y y_used y_out0 y_out1"
        MIX = " ctx_in ctx_n x1 x_ready"
        F = [sems("f0", FRONT + " h hl_used hw hwt_ps hwt"), sems("f1", FRONT + MIX + " y_sel sq nsqrt mask"),
             sems("f2", "x_in out" + MIX)]
        AN = ("a_ready a_used mm mrow mload s_ready e_done pv_done cx cx_free cx_out0 cx_out1 den rden rden_out "
              "load0 load1 load2")
        A = [sems(f"a{l}", AN) for l in range(2)]
        SOFT = ("in", "x_in", "ctx_in", "cx_out0", "cx_out1", "den", "rden_out")
        counted = [s for group in (D, *F, *A) for n, s in group.items() if n not in SOFT]

        block = ctx.enter_context(nc.Block())

        @block.sync
        def _(sp):
            sp.dma_start(cst[:, :], consts).then_inc(s_cst, DMA)
            sp.dma_start(shf[:, :], shifts.partition_broadcast(P)).then_inc(s_cst, DMA)
            sp.dma_start(qwt[:, :, :, :], qweight.rearrange("(k p) e w -> p k e w", p=P)).then_inc(D["qw"], DMA)
            sp.dma_start(wo[:, 0], ow0.rearrange("(k p) n -> p k n", p=P)).then_inc(s_wo, DMA)
            sp.dma_start(wo[:, 1], ow1.rearrange("(k p) n -> p k n", p=P)).then_inc(s_wo, DMA)

            def chunk_stores(l, i, b, c):
                S = F[l]
                for ot in range(QKT):
                    sp.wait_ge(S["qk_3"], ONE + QKT * i + ot + 1)
                    parts = (qp if ot < KT else kp)[l]
                    dst = parts[:, bass.ds(b * DIM + ot % KT * P, P), bass.ds(c * CHUNK, CHUNK)]
                    sp.dma_start(dst.rearrange("c p t -> p c t"), qs[:, ot % 2]).then_inc(S[f"qk_out{ot % 2}"], DMA)
                if l == 0:
                    sp.wait_ge(D["code"], ONE + 2 * (i + 1))
                    for j in range(4):
                        dst = coded[bass.ds(i, 1), :, :, j].rearrange("k a o c i -> (k a o) c i")
                        sp.dma_start(dst, codeb[32 * j:32 * (j + 1)]).then_inc(D["code_out"], DMA)
                for t in range(TT):
                    sp.wait_ge(S["v_used"], ONE + TT * i + t + 1)
                    dst = vp[l][bass.ds(b * QUADS, QUADS), bass.ds(c * CHUNK + t * P, P), :]
                    sp.dma_start(dst.rearrange("s p w -> p s w"),
                                 vt[:, t % 2].rearrange("p (s h) w -> p s (h w)", s=QUADS))\
                      .then_inc(S[f"v_out{t % 2}"], DMA)
                for t in range(TT):
                    sp.wait_ge(S["y_used"], ONE + TT * i + t + 1)
                    sp.dma_start(resd[l][bass.ds(i * CHUNK + t * P, P), :], rt[:, t % 2])\
                      .then_inc(S[f"y_out{t % 2}"], DMA)

            def stored(l, n):
                S = F[l]
                for q in ("qk_out0", "qk_out1"):
                    sp.wait_ge(S[q], ONE + DMA * n * QKT // 2)
                for q in ("v_out0", "v_out1", "y_out0", "y_out1"):
                    sp.wait_ge(S[q], ONE + DMA * n * TT // 2)

            def load(l, it, st):
                s = A[l][f"load{st}"]
                for parts, stage, rows in ((qp[l], qst, Q_ROWS), (kp[l], kst, K_ROWS)):
                    for n, part in enumerate(rows):
                        src = parts[part, bass.ds(it * QUAD * HD, QUAD * HD), :]
                        sp.dma_start(stage[st][n * HD:(n + 1) * HD], src.rearrange("(h d) t -> d h t", d=HD))\
                          .then_inc(s, DMA)
                src = vp[l][bass.ds(it, 1)].rearrange("o (k p) w -> p (o k) w", p=P)
                sp.dma_start(vst[st], src).then_inc(s, DMA)

            def front_stores(l):
                sp.wait_ge(s_ones, 1 + 4 * l)
                for b in range(BATCH):
                    with sp.Fori(0, NCH) as c:
                        chunk_stores(l, b * NCH + c, b, c)
                    if b == 0:
                        stored(l, NCH)
                        if l:
                            sp.wait_ge(A[0]["pv_done"], ONE + len(GROUPS[0]) * STEPS)
                        load(l, 0, 0)
                stored(l, CHUNKS)

            def table_loads():
                sp.wait_ge(D["code_out"], ONE + 4 * DMA * KT)

                def one(ot, pos):
                    a, r = pos % 2, POS * ot + pos
                    if not (type(ot) is int and r < 2):
                        sp.wait_ge(D["wsum"], ONE + r - 1)
                    rows = coded[bass.ds(ot, 1), pos].rearrange("k o j c i -> (k o) (j c i)")
                    sp.dma_start(rep[:, a].rearrange("p j c i -> p (j c i)"),
                                 rows.unsqueeze(1).to_broadcast([GO, NIB, 4 * 2 * DIM])).then_inc(D["in"][a], DMA)
                    for dst, src in ((bd8s, bd8), (bd4s, bd4)):
                        sp.dma_start(dst[:, a], src[bass.ds(ot * POS + pos, 1)].rearrange("o p j m -> p (o j) m"))\
                          .then_inc(D["in"][a], DMA)

                for pos in range(POS):
                    one(0, pos)
                with sp.Fori(1, KT) as ot:
                    for pos in range(POS):
                        one(ot, pos)

            def attention_loads(l):
                S, nb = A[l], len(GROUPS[l])

                def max_rows(it, st):
                    sp.wait_ge(S["mrow"], ONE + it + 1)
                    for n in range(2):
                        r = SROWS + n
                        sp.dma_start(qst[st][r:r + 1].rearrange("o h (q t) -> o (h q) t", t=P), mrow[:, n, :])\
                          .then_inc(S["mload"], DMA)

                load(l, 1, 1)
                if l == 0:
                    sp.wait_ge(D["wt_used"], ONE + 2 * KT * KT)
                load(l, 2, 2)
                max_rows(0, 0)
                rounds = (STEPS - 1) // NSTAGE

                def after(it, r, more):
                    max_rows(it + 1, (r + 1) % NSTAGE)
                    if more:
                        sp.wait_ge(S["pv_done"], ONE + nb * (it + 1))
                        load(l, it + NSTAGE, r)

                with sp.Fori(0, rounds - 1) as u:
                    for r in range(NSTAGE):
                        after(u * NSTAGE + r, r, True)
                for it in range(NSTAGE * (rounds - 1), STEPS - 1):
                    after(it, it % NSTAGE, it + NSTAGE < STEPS)

            front_stores(0)
            table_loads()
            attention_loads(0)
            front_stores(1)
            attention_loads(1)
            S = F[2]
            with sp.Fori(0, CHUNKS) as i:
                for t in range(TT):
                    sp.wait_ge(S["x_ready"], ONE + TT * i + t + 1)
                    sp.dma_start(out[bass.ds(i * CHUNK + t * P, P), :], xb[:, t]).then_inc(S["out"], DMA)
            sp.wait_ge(S["out"], ONE + DMA * TT * CHUNKS)

        @block.gpsimd
        def _(pool):
            pool.dma_start(xb, x[0:CHUNK, :].rearrange("(t p) d -> p t d", p=P)).then_inc(F[0]["x_in"], DMA)
            for n, a in enumerate((ob0, bbase, ob1, bffn)):
                pool.dma_start(rbp[:, n // 2, n % 2], a.partition_broadcast(P)).then_inc(s_rb, DMA)
            pool.memset(vt[:, :, :, HD:], 1.0).then_inc(s_ones, 1)

            def context(l, i):
                S, pl = F[l], l - 1
                b, c = i // NCH, i % NCH
                cols = slice(c * CHUNK, (c + 1) * CHUNK)
                pool.wait_ge(A[pl]["rden_out"], DMA * QUADS * (b + 1))
                pool.wait_ge(S["x1"], ONE + TT * i)
                src = ctxd[pl][b * DIM:(b + 1) * DIM, cols]
                pool.dma_start(cxn, src.rearrange("(k p) t -> p k t", p=P)).then_inc(S["ctx_in"], DMA)
                for k in range(KT):
                    h = P // HD
                    src = rdend[pl][b * HEADS + k * h:b * HEADS + (k + 1) * h, cols]
                    pool.dma_start(rdr[:, k], src.unsqueeze(1).to_broadcast([h, HD, CHUNK])).then_inc(S["ctx_in"], DMA)

            def rows(l, i):
                S = F[l]
                if l == 2:
                    pool.wait_ge(S["out"], ONE + DMA * TT * i)
                else:
                    pool.wait_ge(S["xn"], ONE + TT * i)
                src = (x if l == 0 else resd[l - 1])[i * CHUNK:(i + 1) * CHUNK, :]
                pool.dma_start(xb, src.rearrange("(t p) d -> p t d", p=P)).then_inc(S["x_in"], DMA)

            def residual(l, i):
                S = F[l]
                if l == 0:
                    pool.wait_ge(S["x_in"], DMA * (i + 1))
                else:
                    pool.wait_ge(S["x_ready"], ONE + TT * (i + 1))
                pool.wait_ge(S["y_used"], ONE + TT * i)
                for t in range(TT):
                    pool.tensor_tensor(xr[:, t], xb[:, t], rb[:, l], ALU.add).then_inc(S["xr"], 1)
                pool.wait_ge(S["xr"], ONE + TT * (i + 1))

            def front(l):
                for i in range(CHUNKS):
                    if i + 1 < CHUNKS and l:
                        context(l, i + 1)
                    residual(l, i)
                    if i + 1 < CHUNKS:
                        rows(l, i + 1)

            def stage_ones(l, st):
                pool.memset(kst[st][SROWS:BROWS], 1.0).then_inc(s_ones, 1)

            def stored(l):
                S = F[l]
                for n in ("qk_out0", "qk_out1"):
                    pool.wait_ge(S[n], ONE + DMA * CHUNKS * QKT // 2)
                for n in ("v_out0", "v_out1", "y_out0", "y_out1"):
                    pool.wait_ge(S[n], ONE + DMA * CHUNKS * TT // 2)

            def attention(l):
                S = A[l]

                def context_store(it, qh):
                    pool.wait_ge(S["cx"], ONE + 2 * it + qh + 1)
                    cols = slice(qh * CHUNK, (qh + 1) * CHUNK)
                    for j in range(QUAD):
                        pool.dma_start(ctxd[l][bass.ds(it * QUAD * HD + j * HD, HD), cols],
                                       cx[32 * j:32 * j + HD, qh]).then_inc(S[f"cx_out{qh}"], DMA)
                    pool.dma_start(dend[l][bass.ds(it * QUAD, QUAD), cols], cx[HD:P:32, qh])\
                        .then_inc(S[f"cx_out{qh}"], DMA)

                dense = lambda d, it: d[bass.ds(it * QUAD, QUAD), :].rearrange("r (a t) -> (r a) t", t=DW)

                def reciprocal_store(it):
                    pool.wait_ge(S["rden"], ONE + it + 1)
                    pool.dma_start(dense(rdend[l], it), dno[:, :]).then_inc(S["rden_out"], DMA)

                def denominators(it):
                    for qh in range(QHS):
                        pool.wait_ge(S[f"cx_out{qh}"], 5 * DMA * (it + 1))
                    pool.sem_inc(S["cx_free"], 1)
                    if type(it) is not int or it:
                        reciprocal_store(it - 1)
                    pool.dma_start(dni[:, :], dense(dend[l], it)).then_inc(S["den"], DMA)

                def one(it):
                    for qh in range(QHS):
                        context_store(it, qh)
                    denominators(it)

                one(0)
                with pool.Fori(1, STEPS - 1) as it:
                    one(it)
                pool.wait_ge(S["pv_done"], ONE + len(GROUPS[l]) * (STEPS - 1))
                context(l + 1, 0)
                rows(l + 1, 0)
                one(STEPS - 1)
                reciprocal_store(STEPS - 1)

            pool.wait_ge(s_prep, 6)
            front(0)
            stage_ones(0, 0)
            stored(0)
            stage_ones(0, 1)
            w = lambda a: a.rearrange("(k p) n -> p k n", p=P)
            for n, a in enumerate((wq1, wk1, wv1)):
                pool.dma_start(wqkv[:, :, n * DIM:(n + 1) * DIM], w(a)).then_inc(s_w1, DMA)
            pool.wait_ge(D["wt_used"], ONE + 2 * KT * KT)
            stage_ones(0, 2)
            attention(0)
            pool.wait_ge(A[0]["pv_done"], ONE + len(GROUPS[0]) * STEPS)
            pool.memset(vt[:, :, :, HD:], 1.0).then_inc(s_ones, 1)
            front(1)
            stored(1)
            stage_ones(1, 1)
            stage_ones(1, 2)
            attention(1)
            for i in range(1, CHUNKS):
                context(2, i)
                rows(2, i)

        @block.scalar
        def _(act):
            copy = lambda o, i: act.activation(o, i, ACT.Copy)
            w = lambda a: a.rearrange("(k p) n -> p k n", p=P)
            ER = EXPERTS * RANK
            for s, dst, src in ((s_wrl, wrl[:, :, 0:ER], w(lora_a)), (s_wrl, wrl[:, :, ER:], w(wrout)),
                                (s_wrl, brt[:, :], brout.partition_broadcast(P)),
                                (s_wqk, bqk[:, 0], bqk0), (s_wqk, bqk[:, 1], bqk1),
                                (s_wqk, wqkv[:, :, 0:2 * DIM], w(qkvw)[:, :, 0:2 * DIM]),
                                (s_wv, wqkv[:, :, 2 * DIM:], w(qkvw)[:, :, 2 * DIM:]),
                                (s_wv, bv[:, 0], bv0.partition_broadcast(P)),
                                (s_wv, bv[:, 1], bv1.partition_broadcast(P)),
                                (s_wy, wff[:, :, :], w(wbase)), (s_wy, lb[:, :], lora_b)):
                act.dma_start(dst, src).then_inc(s, DMA)
            for s in counted[::2]:
                act.sem_inc(s, ONE)
            act.wait_ge(s_cst, 2 * DMA)
            for o, c in ((idb, C_ID), (upb, C_UP), (lob, C_LO)):
                copy(o[:, :], cst[:, c:c + P]).then_inc(s_prep, 1)

            def deviation(l, i):
                S = F[l]
                act.wait_ge(S["stat"], ONE + (TT + 1) * (i + 1))
                act.activation(std[:, :], mv[:, 1], ACT.Sqrt, bias=eps_col[:, :]).then_inc(S["sqrt"], 1)

            def front(l):
                S = F[l]
                if l == 0:
                    act.wait_ge(s_prep, 4)
                deviation(l, 0)
                if l == 0:
                    act.wait_ge(s_wqk, 3 * DMA)

                def chunk(i, more):
                    for t in range(TT):
                        act.wait_ge(S["tp"], ONE + TT * i + t + 1)
                        if t == 0:
                            act.wait_ge(S["y"], ONE + TT * i)
                        copy(xnt[:, :, t * P:(t + 1) * P], banks[t % 2].rearrange("p (k q) -> p k q", k=KT))\
                            .then_inc(S["xnt"], 1)
                    for ot in range(QKT):
                        n = QKT * i + ot
                        act.wait_ge(S["qk"], ONE + n + 1)
                        act.wait_ge(S["qk_r"], ONE + (QKT * i if ot < 2 else n - 1))
                        act.wait_ge(S[f"qk_out{ot % 2}"], ONE + DMA * (QKT // 2 * i + ot // 2))
                        src, b = banks[4 + ot % 2], bqk[:, l, ot:ot + 1]
                        act.activation(qf[:, ot % 2], src, ACT.Identity, bias=b).then_inc(S["qk_f"], 1)
                        act.activation(qs[:, ot % 2, 0], src, ACT.Identity, bias=b).then_inc(S["qk_f"], 1)
                        if l and ot == 1:
                            for t in range(TT):
                                act.wait_ge(S["xn"], ONE + TT * i + t + 1)
                                act.wait_ge(S["sq"], ONE + TT * i + t)
                                act.activation(junk, xn[:, t], ACT.Square, accum_out=nrm[:, 0, t:t + 1])\
                                    .then_inc(S["sq"], 1)
                        if ot == LN_STATS:
                            if l:
                                act.wait_ge(S["sq"], ONE + TT * (i + 1))
                                act.activation(nrm[:, 1], nrm[:, 0], ACT.Sqrt).then_inc(S["nsqrt"], 1)
                            if more:
                                deviation(l, i + 1)
                        if l == 0 and ot == QKT - 2:
                            act.wait_ge(S["hwt_ps"], ONE + i + 1)
                            copy(hwt, banks[3].rearrange("p (t q) -> p t q", t=TT)).then_inc(S["hwt"], 1)
                    for t in range(TT if l else 0):
                        n = TT * i + t
                        act.wait_ge(S["mask"], ONE + 2 * (i + 1))
                        act.wait_ge(S["y"], ONE + n + 1)
                        act.wait_ge(S["y_used"], ONE + (TT * i if t < 2 else n - 1))
                        act.activation(ysel[:, t % 2], banks[6 if t % 2 == 0 else 2], ACT.Copy,
                                       scale=nrm[:, 3, t:t + 1]).then_inc(S["y_sel"], 1)

                with act.Fori(0, CHUNKS - 1) as i:
                    chunk(i, True)
                chunk(CHUNKS - 1, False)

            def tables():
                with act.Fori(0, KT) as ot:
                    for n in range(2):
                        act.wait_ge(D["wl"] if n == 0 else D["wsum"], ONE + POS * (ot + 1))
                        act.wait_ge(D["wt_used"], ONE + 2 * KT * ot)
                        copy(wrow[:, n], banks[4 + n]).then_inc(D["wrow"], 1)
                        for k in range(KT):
                            act.wait_ge(D["wt"], ONE + 2 * KT * ot + KT * n + k + 1)
                            copy((w4, w8)[n][:, k, bass.ds(ot * P, P)], banks[6 + k % 2][:, 0:P]).then_inc(D["wt_used"], 1)

            def attention(l):
                S, groups = A[l], GROUPS[l]
                nb = len(groups)

                def one(it):
                    first = 0
                    for g, (qh, kt, off, last) in enumerate(groups):
                        for p in range(2):
                            act.wait_ge(S["s_ready"], ONE + 2 * nb * it + 2 * g + p + 1)
                            if p == 0:
                                act.wait_ge(S["pv_done"], ONE + nb * it + max(0, g - 1))
                            act.activation(pr[:, g % 2, 2 * p:2 * p + 2, off:], pair[p][:, :, off:], ACT.Exp,
                                           scale=SCALE).then_inc(S["e_done"], 1)
                        done = [n for n, q in enumerate(groups) if q[3]]
                        if g == done[0] + 1:
                            evacuate(it, 0, done[0])
                    evacuate(it, 1, done[1])

                def evacuate(it, qh, g):
                    act.wait_ge(S["pv_done"], ONE + nb * it + g + 1)
                    act.wait_ge(S["cx_free"], ONE + it)
                    copy(cx[:, qh], banks[RING]).then_inc(S["cx"], 1)

                with act.Fori(0, STEPS) as it:
                    one(it)

            front(0)
            tables()
            attention(0)
            front(1)
            attention(1)

        @block.vector
        def _(dve):
            before = [0]

            dve.memset(eps_col[:, :], EPS).then_inc(s_prep, 1)

            def look_ups():
                def one_hot(ot, pos):
                    a, r = pos % 2, POS * ot + pos
                    dve.wait_ge(D["in"][a], ONE + 3 * DMA * (POS // 2 * ot + pos // 2 + 1))
                    dve.wait_ge(D["wl"], ONE + (r - 1 if pos else r))
                    dve.tensor_scalar(oh[:, a], rep[:, a, :, 0], kcol, None, ALU.is_equal).then_inc(D["oh"], 1)

                def masks(ot, pos):
                    a, r = pos % 2, POS * ot + pos
                    dve.wait_ge(D["wsum"], ONE + (r - 1 if pos else r))
                    for j in range(4):
                        dve.wait_ge(D["tab"], ONE + 4 * r + j + 1)
                        dve.scalar_tensor_tensor(out=msk[:, a, j], in0=rep[:, a, j, 1], scalar=kcol, in1=banks[j],
                                                 op0=ALU.is_equal, op1=ALU.mult).then_inc(D["msk"], 1)

                def tile(ot, more):
                    for pos in range(POS):
                        if pos + 1 < POS:
                            one_hot(ot, pos + 1)
                        masks(ot, pos)
                        if pos + 1 == POS and more:
                            one_hot(ot + 1, 0)

                one_hot(0, 0)
                with dve.Fori(0, KT - 1) as ot:
                    tile(ot, True)
                tile(KT - 1, False)

            dve.wait_ge(s_rb, 4 * DMA)
            for l in range(2):
                dve.tensor_tensor(rb[:, l], rbp[:, l, 0], rbp[:, l, 1], ALU.add).then_inc(s_prep, 1)

            def context(l, i):
                S = F[l]
                dve.wait_ge(S["ctx_in"], DMA * (1 + KT) * (i + 1))
                dve.tensor_tensor(cxn, cxn, rdr, ALU.mult).then_inc(S["ctx_n"], 1)

            def mix(l, i):
                S = F[l]
                dve.wait_ge(S["x_in"], DMA * (i + 1))
                for t in range(TT):
                    dve.wait_ge(S["x1"], ONE + TT * i + t + 1)
                    dve.tensor_tensor(xb[:, t], banks[2 + t % 2], xb[:, t], ALU.add).then_inc(S["x_ready"], 1)

            def sparsemax(then):
                srt, cum, kz, sup, sel, w = (sm[:, n] for n in range(6))
                k4 = karr.unsqueeze(1).to_broadcast([P, TT, EXPERTS])
                for t in range(TT):
                    then(dve.max(srt[:, t], lg[:, t]), wait=t == TT - 1)
                then(dve.tensor_copy(cum[:, :, 0:1], srt[:, :, 0:1]))
                for e in range(1, EXPERTS):
                    then(dve.tensor_tensor(cum[:, :, e:e + 1], cum[:, :, e - 1:e], srt[:, :, e:e + 1], ALU.add))
                then(dve.tensor_tensor(kz, srt, k4, ALU.mult))
                then(dve.tensor_scalar(kz, kz, 1.0, None, ALU.add))
                then(dve.tensor_tensor(sup, kz, cum, ALU.is_gt))
                then(dve.reduce_sum(sc[:, 0], sup, AX))
                kb = sc[:, 0].unsqueeze(2).to_broadcast([P, TT, EXPERTS])
                then(dve.tensor_tensor(sel, k4, kb, ALU.is_equal))
                then(dve.tensor_tensor(sel, sel, cum, ALU.mult))
                then(dve.reduce_sum(sc[:, 1], sel, AX))
                then(dve.tensor_scalar(sc[:, 1], sc[:, 1], -1.0, None, ALU.add))
                then(dve.reciprocal(sc[:, 2], sc[:, 0]))
                then(dve.tensor_tensor(sc[:, 3], sc[:, 1], sc[:, 2], ALU.mult))
                tb = sc[:, 3].unsqueeze(2).to_broadcast([P, TT, EXPERTS])
                then(dve.tensor_tensor(w, lg[:, :, :], tb, ALU.subtract))
                then(dve.tensor_scalar(w, w, 0.0, None, ALU.max))
                return w

            def statistics(l, i, then):
                S = F[l]
                if l:
                    dve.wait_ge(S["x_ready"], ONE + TT * (i + 1))
                else:
                    dve.wait_ge(S["x_in"], DMA * (i + 1))
                for t in range(TT):
                    dve.bn_stats(stats[:, t], xb[:, t]).then_inc(S["stat"], 1)
                dve.wait_ge(S["stat"], ONE + (TT + 1) * i + TT)
                (em, es), (om, os_) = ((stats[:, :, n], stats[:, :, n + 1]) for n in (1, 4))
                mean, var, dif, dev = (mv[:, n] for n in range(4))
                then(dve.tensor_tensor(mean, em, om, ALU.add), wait=False)
                then(dve.tensor_tensor(dif, em, om, ALU.subtract), wait=False)
                then(dve.tensor_tensor(dev, es, os_, ALU.add))
                then(dve.tensor_scalar(mean, mean, 0.5, None, ALU.mult), wait=False)
                then(dve.tensor_tensor(dif, dif, dif, ALU.mult))
                then(dve.tensor_scalar(dif, dif, 0.25, None, ALU.mult), wait=False)
                then(dve.tensor_scalar(dev, dev, 1.0 / DIM, None, ALU.mult))
                dve.tensor_tensor(var, dif, dev, ALU.add).then_inc(S["stat"], 1)

            def normalise(l, i, then):
                S = F[l]
                dve.wait_ge(S["sqrt"], ONE + i + 1)
                then(dve.reciprocal(rstd[:, :], std[:, :]))
                dve.wait_ge(S["tp"], ONE + TT * i)
                if l:
                    dve.wait_ge(S["sq"], ONE + TT * i)
                for t in range(TT):
                    dve.tensor_scalar(xn[:, t], xb[:, t], mv[:, 0, t:t + 1], rstd[:, t:t + 1], ALU.subtract, ALU.mult)\
                       .then_inc(S["xn"], 1)

            def code_plane(i, e, then):
                c, s = e // 4, e % 4
                shape = [P, WORDS, BITS]
                v = lambda a: a.rearrange("p (w b) -> p w b", w=WORDS)
                if e == 0:
                    dve.wait_ge(D["code_out"], ONE + 4 * DMA * i)
                plane = qwt[:, bass.ds(i, 1), e, :].rearrange("p k w -> p (k w)")
                then(dve.tensor_tensor(v(bits), plane.unsqueeze(2).to_broadcast(shape),
                                       shf[:, :].unsqueeze(1).to_broadcast(shape), ALU.logical_shift_right))
                then(dve.tensor_scalar(half[c] if s == 0 else bits2, bits, 1, s, ALU.bitwise_and,
                                       ALU.logical_shift_left))
                if s:
                    then(dve.tensor_tensor(half[c], half[c], bits2, ALU.bitwise_or))
                if s == 3:
                    dve.tensor_copy(codeb[:, c], half[c]).then_inc(D["code"], 1)

            def front(l):
                S = F[l]
                per = CHAIN[l]
                first = Then(dve, step, before[0], 0, 8)
                if l:
                    mix(l, 0)
                statistics(l, 0, first)
                normalise(l, 0, first)
                base = before[0] + 8
                if l == 0:
                    dve.wait_ge(s_wrl, 3 * DMA)
                    dve.wait_ge(s_wv, 3 * DMA)
                    dve.wait_ge(s_cst, 2 * DMA)
                    dve.wait_ge(D["qw"], ONE + DMA)

                def chunk(i, more):
                    then = Then(dve, step, base, i, per)
                    if l == 0:
                        dve.wait_ge(S["h"], ONE + 2 * i + 2)
                        dve.tensor_tensor(lg[:, :, :], banks[3][:, 0:TT * EXPERTS].rearrange("p (t e) -> p t e", t=TT),
                                          brt[:, :].unsqueeze(1).to_broadcast([P, TT, EXPERTS]), ALU.add)\
                           .then_inc(S["hl_used"], 1)
                        dve.wait_ge(S["hl_used"], ONE + 2 * i + 1)
                        dve.tensor_copy(hs.rearrange("p t e r -> p (t e r)"), banks[2]).then_inc(S["hl_used"], 1)
                        w = sparsemax(then)
                        for t in range(TT):
                            dve.tensor_tensor(hw[:, t], hs[:, t], w[:, t].unsqueeze(2).to_broadcast([P, EXPERTS, RANK]),
                                              ALU.mult).then_inc(S["hw"], 1)
                    elif more:
                        context(l, i + 1)
                    for ot in range(QKT):
                        n = QKT * i + ot
                        a = ot % 2
                        dve.wait_ge(S["qk_f"], ONE + 2 * (n + 1))
                        dve.tensor_tensor(qr[:, a], qf[:, a], qs[:, a, 0], ALU.subtract).then_inc(S["qk_r"], 1)
                        dve.wait_ge(S["qk_r"], ONE + n + 1)
                        then(dve.tensor_copy(qs[:, a, 1], qr[:, a]))
                        dve.tensor_tensor(qs[:, a, 2], qr[:, a], qs[:, a, 1], ALU.subtract).then_inc(S["qk_3"], 1)
                        if l == 0:
                            code_plane(i, ot, then)
                        if more:
                            if l and ot == PROJECT:
                                mix(l, i + 1)
                            if ot == LN_STATS:
                                statistics(l, i + 1, then)
                            if ot == LN_STATS + 1:
                                normalise(l, i + 1, then)
                        if l and ot == LN_STATS + 1:
                            dve.wait_ge(S["nsqrt"], ONE + i + 1)
                            dve.tensor_scalar(nrm[:, 2], nrm[:, 1], NORM_T, None, ALU.is_gt).then_inc(S["mask"], 1)
                            dve.tensor_scalar(nrm[:, 3], nrm[:, 1], NORM_T, None, ALU.is_le).then_inc(S["mask"], 1)
                    for t in range(TT):
                        n = TT * i + t
                        dve.wait_ge(S["v"], ONE + n + 1)
                        dve.wait_ge(S[f"v_out{t % 2}"], ONE + DMA * (TT // 2 * i + t // 2))
                        h3 = lambda a: a.rearrange("p (h d) -> p h d", h=HEADS)
                        dve.tensor_tensor(vt[:, t % 2, :, 0:HD], h3(banks[6 + t % 2]), h3(bv[:, l]), ALU.add)\
                           .then_inc(S["v_used"], 1)
                    dve.wait_ge(S["xr"], ONE + TT * (i + 1))
                    for t in range(TT):
                        n = TT * i + t
                        dve.wait_ge(S["y"], ONE + n + 1)
                        dve.wait_ge(S[f"y_out{t % 2}"], ONE + DMA * (TT // 2 * i + t // 2))
                        if l == 0:
                            dve.tensor_tensor(rt[:, t % 2], banks[6 + t % 2], xr[:, t], ALU.add).then_inc(S["y_used"], 1)
                        else:
                            dve.wait_ge(S["y_sel"], ONE + n + 1)
                            then(dve.scalar_tensor_tensor(out=ysel[:, t % 2], in0=banks[7 if t % 2 == 0 else 3],
                                                          scalar=nrm[:, 2, t:t + 1], in1=ysel[:, t % 2],
                                                          op0=ALU.mult, op1=ALU.add))
                            dve.tensor_tensor(rt[:, t % 2], ysel[:, t % 2], xr[:, t], ALU.add).then_inc(S["y_used"], 1)
                    assert then.n == (per if more else per - 8), then.n

                with dve.Fori(0, CHUNKS - 1) as i:
                    chunk(i, True)
                chunk(CHUNKS - 1, False)
                before[0] = base + per * CHUNKS - 8

            def attention(l):
                S, units = A[l], UNITS[l]
                na = len(units)
                base = before[0]

                def maxima(it):
                    for k, (h, qt, hf, only, k0, n) in enumerate(units):
                        dve.wait_ge(S["a_ready"], ONE + (na + 1) * it + k + 1)
                        o = mmx[:, h, qt:qt + 1] if only else mx[:, hf, h, qt:qt + 1]
                        dve.reduce_max(o, banks[k % RING][:, 0:n], AX).then_inc(S["a_used"], 1)
                    dve.wait_ge(S["a_used"], ONE + na * (it + 1))
                    q0 = min(qt for _, qt, _, only, _, _ in units if not only)
                    dve.tensor_tensor(mmx[:, :, q0:], mx[:, 0, :, q0:], mx[:, 1, :, q0:], ALU.max).then_inc(S["mm"], 1)
                    dve.wait_ge(S["a_ready"], ONE + (na + 1) * (it + 1))
                    dve.wait_ge(S["mload"], ONE + 2 * DMA * it)
                    rows = banks[na % RING][0:QUAD * QT, 0:P]
                    dve.tensor_scalar(mrow[:, 0], rows, -1.0, None, ALU.mult).then_inc(step, 1)
                    dve.wait_ge(step, base + it + 1)
                    dve.scalar_tensor_tensor(out=mrow[:, 1], in0=rows, scalar=-1.0, in1=mrow[:, 0],
                                             op0=ALU.mult, op1=ALU.subtract).then_inc(S["mrow"], 1)

                def reciprocals(it):
                    dve.wait_ge(S["den"], DMA * (it + 1))
                    if type(it) is not int or it:
                        dve.wait_ge(S["rden_out"], DMA * it)
                    dve.reciprocal(dno[:, :], dni[:, :]).then_inc(S["rden"], 1)

                maxima(0)
                maxima(1)
                maxima(2)
                reciprocals(0)
                with dve.Fori(3, STEPS) as it:
                    maxima(it)
                    reciprocals(it - 2)
                before[0] = base + STEPS
                reciprocals(STEPS - 2)
                context(l + 1, 0)
                reciprocals(STEPS - 1)

            front(0)
            look_ups()
            attention(0)
            front(1)
            attention(1)
            mix(2, 0)
            with dve.Fori(1, CHUNKS) as i:
                context(2, i)
                mix(2, i)

        @block.tensor
        def _(pe):
            def product(o, pairs, start=True, stop=True):
                for n, (a, b) in enumerate(pairs):
                    last = pe.matmul(o, a, b, start=start and n == 0, stop=stop and n == len(pairs) - 1)
                return last

            for s in counted[1::2]:
                pe.sem_inc(s, ONE)

            def tables():
                def pick(ot, pos):
                    a, r = pos % 2, POS * ot + pos
                    pe.wait_ge(D["in"][a], ONE + 3 * DMA * (POS // 2 * ot + pos // 2 + 1))
                    pe.wait_ge(D["oh"], ONE + r + 1)
                    for j in range(4):
                        pe.wait_ge(D["msk"], ONE + (4 * (r - 1) + j + 1 if pos else 4 * r))
                        product(banks[j], [(bd8s[:, a, j], oh[:, a, j])]).then_inc(D["tab"], 1)
                    if pos == 0:
                        pe.wait_ge(D["wrow"], ONE + 2 * ot)
                    for j in range(4):
                        last = product(banks[4][32 * j:32 * j + 32], [(bd4s[:, a, j], oh[:, a, j])],
                                       start=pos == 0, stop=pos == POS - 1)
                    last.then_inc(D["wl"], 1)

                def add_up(ot, pos):
                    a, r = pos % 2, POS * ot + pos
                    for j in range(4):
                        pe.wait_ge(D["msk"], ONE + 4 * r + j + 1)
                        last = product(banks[5][32 * j:32 * j + 32],
                                       [(cst[:, C_SEL + 32 * pos:C_SEL + 32 * pos + 32], msk[:, a, j])],
                                       start=pos == 0, stop=pos == POS - 1)
                    last.then_inc(D["wsum"], 1)

                def turn(ot, n):
                    pe.wait_ge(D["wrow"], ONE + 2 * ot + n + 1)
                    for k in range(KT):
                        m = KT * n + k
                        pe.wait_ge(D["wt_used"], ONE + 2 * KT * ot + (m - 1 if m >= 2 else 0))
                        pe.transpose(banks[6 + k % 2][:, 0:P], wrow[:, n, k * P:(k + 1) * P], ident)\
                          .then_inc(D["wt"], 1)

                with pe.Fori(0, KT) as ot:
                    for pos in range(POS):
                        pick(ot, pos)
                        if pos:
                            add_up(ot, pos - 1)
                    turn(ot, 0)
                    add_up(ot, POS - 1)
                    turn(ot, 1)

            def project(l, i):
                S = F[l]
                pe.wait_ge(S["ctx_n"], ONE + i + 1)
                for t in range(TT):
                    n = TT * i + t
                    if t >= 2:
                        pe.wait_ge(S["x_ready"], ONE + n - 1)
                    elif l == 2:
                        pe.wait_ge(S["x_ready"], ONE + TT * i)
                    elif type(i) is not int:
                        pe.wait_ge(S["y_used"], ONE + TT * (i - 1))
                    product(banks[2 + t % 2], [(cxn[:, k, t * P:(t + 1) * P], wo[:, l - 1, k]) for k in range(KT)])\
                        .then_inc(S["x1"], 1)

            def front(l):
                S = F[l]
                ER = EXPERTS * RANK

                def chunk(i, more):
                    for t in range(TT):
                        n = TT * i + t
                        pe.wait_ge(S["xn"], ONE + n + 1)
                        pe.wait_ge(S["xnt"], ONE + (n - 1 if t >= 2 else TT * i))
                        for k in range(KT):
                            last = pe.transpose(banks[t % 2][:, k * P:(k + 1) * P], xn[:, t, k * P:(k + 1) * P], ident)
                        last.then_inc(S["tp"], 1)
                    pe.wait_ge(S["xnt"], ONE + TT * (i + 1))
                    tok = lambda k, t: xnt[:, k, t * P:(t + 1) * P]
                    if l == 0:
                        pe.wait_ge(s_wrl, 3 * DMA)
                        pe.wait_ge(S["hl_used"], ONE + 2 * i)
                        for t in range(TT):
                            last = product(banks[2][:, t * ER:(t + 1) * ER],
                                           [(tok(k, t), wrl[:, k, 0:ER]) for k in range(KT)])
                        last.then_inc(S["h"], 1)
                        pe.wait_ge(S["hwt"], ONE + i)
                        for t in range(TT):
                            last = product(banks[3][:, t * EXPERTS:(t + 1) * EXPERTS],
                                           [(tok(k, t), wrl[:, k, ER:]) for k in range(KT)])
                        last.then_inc(S["h"], 1)
                        pe.wait_ge(s_wqk, 3 * DMA)
                    for ot in range(QKT):
                        n = QKT * i + ot
                        pe.wait_ge(S["qk_f"], ONE + (2 * (n - 1) if ot >= 2 else 2 * QKT * i))
                        product(banks[4 + ot % 2], [(wqkv[:, k, ot * P:(ot + 1) * P], xnt[:, k]) for k in range(KT)])\
                            .then_inc(S["qk"], 1)
                        if l and more and ot == PROJECT:
                            project(l, i + 1)
                        if l == 0 and ot == LN_STATS:
                            pe.wait_ge(S["hw"], ONE + TT * (i + 1))
                            for t in range(TT):
                                last = pe.transpose(banks[3][:, t * P:(t + 1) * P],
                                                    hw[:, t].rearrange("p e r -> p (e r)"), ident)
                            last.then_inc(S["hwt_ps"], 1)
                    if l == 0:
                        pe.wait_ge(s_wv, 3 * DMA)
                    for t in range(TT):
                        n = TT * i + t
                        if t >= 2:
                            pe.wait_ge(S["v_used"], ONE + n - 1)
                        else:
                            pe.wait_ge(S["y_used"], ONE + TT * i)
                        product(banks[6 + t % 2], [(tok(k, t), wqkv[:, k, 2 * DIM:]) for k in range(KT)])\
                            .then_inc(S["v"], 1)
                    if l == 0:
                        pe.wait_ge(s_wy, 2 * DMA)
                    if l == 0:
                        pe.wait_ge(S["hwt"], ONE + i + 1)
                    for t in range(TT):
                        n = TT * i + t
                        if t >= 2:
                            pe.wait_ge(S["y_used"], ONE + n - 1)
                        else:
                            pe.wait_ge(S["v_used"], ONE + TT * i + (TT if l else t + 3))
                        if l == 0:
                            product(banks[6 + t % 2], [(tok(k, t), wff[:, k]) for k in range(KT)] + [(hwt[:, t], lb[:, :])])\
                                .then_inc(S["y"], 1)
                        else:
                            lo, hi = (6, 7) if t % 2 == 0 else (2, 3)
                            product(banks[lo], [(tok(k, t), w4[:, k]) for k in range(KT)])
                            product(banks[hi], [(tok(k, t), w8[:, k]) for k in range(KT)]).then_inc(S["y"], 1)

                if l:
                    project(l, 0)
                with pe.Fori(0, CHUNKS - 1) as i:
                    chunk(i, True)
                chunk(CHUNKS - 1, False)

            def attention(l):
                S, units, groups = A[l], UNITS[l], GROUPS[l]
                na, nb, causal = len(units), len(groups), l == 1

                def score_tile(it, st, k):
                    h, qt, _, _, k0, n = units[k]
                    if k < RING:
                        pe.wait_ge(S["a_used"], ONE + na * it)
                        pe.wait_ge(S["mrow"], ONE + it)
                    else:
                        pe.wait_ge(S["a_used"], ONE + na * it + k - RING + 1)
                    diagonal = causal and k0 + n == (qt + 1) * P
                    ins = pe.matmul(banks[k % RING][:, 0:n], qst[st][0:SROWS, h, qt * P:(qt + 1) * P],
                                    kst[st][0:SROWS, h, k0:k0 + n], start=True, stop=not diagonal)
                    if diagonal:
                        ins = pe.matmul(banks[k % RING][:, n - P:n], idb[:, :], upb[:, :], start=False, stop=True)
                    ins.then_inc(S["a_ready"], 1)

                def maxima_rows(it):
                    pe.wait_ge(S["mm"], ONE + it + 1)
                    pe.transpose(banks[na % RING][0:QUAD * QT, 0:P], mmx[:, :, :].rearrange("p h q -> p (h q)"), ident)\
                        .then_inc(S["a_ready"], 1)

                def transposed_scores(it, st, g, p):
                    qh, kt, off, _ = groups[g]
                    pe.wait_ge(S["e_done"], ONE + 2 * nb * it + (2 * g + p - 1 if g else 0))
                    diagonal = causal and kt * P >= qh * CHUNK
                    for n in range(2):
                        h = 2 * p + n
                        ins = pe.matmul(pair[p][:, n, off:], kst[st][0:BROWS, h, kt * P:(kt + 1) * P],
                                        qst[st][0:BROWS, h, qh * CHUNK + off:(qh + 1) * CHUNK],
                                        start=True, stop=not diagonal)
                        if diagonal:
                            ins = pe.matmul(pair[p][:, n, off:off + P], idb[:, :], lob[:, :], start=False, stop=True)
                    ins.then_inc(S["s_ready"], 1)

                def weigh_values(it, st, g):
                    qh, kt, off, last = groups[g]
                    pe.wait_ge(S["e_done"], ONE + 2 * nb * it + 2 * g + 2)
                    if kt == 0:
                        pe.wait_ge(S["cx"], ONE + 2 * it + qh)
                    for j in range(QUAD):
                        ins = pe.matmul(banks[RING][VW * j:VW * (j + 1), off:], vst[st][:, kt, VW * j:VW * (j + 1)],
                                        pr[:, g % 2, j, off:], start=kt == 0, stop=last)
                    ins.then_inc(S["pv_done"], 1)

                def step_(it, st, nxt):
                    tiles = iter(range(na if nxt else 0))

                    def ahead(n):
                        for _, k in list(zip(range(n), tiles)):
                            score_tile(ait, ast, k)
                            if k == na - 1:
                                left.append(LAG)

                    left = []
                    if nxt:
                        ait, ast, loads = nxt
                        pe.wait_ge(S[f"load{ast}"], ONE + LOADS * DMA * loads)
                        ahead(LEAD)
                    pe.wait_ge(S["mload"], ONE + 2 * DMA * (it + 1))
                    for g in range(nb):
                        transposed_scores(it, st, g, 0)
                        ahead(1)
                        transposed_scores(it, st, g, 1)
                        ahead(2 if g % 4 == 0 else 1)
                        if left and left[0] == 0:
                            maxima_rows(ait)
                        left = [n - 1 for n in left]
                        if g:
                            weigh_values(it, st, g - 1)
                        ahead(2)
                    assert not nxt or left[0] < 0
                    weigh_values(it, st, nb - 1)

                pe.wait_ge(F[l]["y_used"], ONE + TT * CHUNKS)
                pe.wait_ge(s_ones, 4 + 3 * l)
                pe.wait_ge(S["load0"], ONE + LOADS * DMA)
                for k in range(na):
                    score_tile(0, 0, k)
                maxima_rows(0)
                with pe.Fori(0, (STEPS - 1) // NSTAGE) as u:
                    for r in range(NSTAGE):
                        it = u * NSTAGE + r
                        step_(it, r, (it + 1, (r + 1) % NSTAGE, u + 1 + (r + 1) // NSTAGE))
                step_(STEPS - 1, (STEPS - 1) % NSTAGE, None)

            pe.wait_ge(s_cst, 2 * DMA)
            front(0)
            pe.wait_ge(F[0]["y_used"], ONE + TT * CHUNKS)
            tables()
            pe.wait_ge(s_prep, 6)
            pe.wait_ge(D["wt_used"], ONE + 2 * KT * KT)
            attention(0)
            pe.wait_ge(s_w1, 3 * DMA)
            pe.wait_ge(s_wo, 2 * DMA)
            pe.wait_ge(A[0]["cx"], ONE + 2 * STEPS)
            front(1)
            attention(1)
            pe.wait_ge(A[1]["cx"], ONE + 2 * STEPS)
            with pe.Fori(0, CHUNKS) as i:
                project(2, i)


def kernel(**inputs):
    import concourse.bacc as _bacc
    from concourse.bass_utils import run_bass_kernel_spmd as _run

    g = {k: np.asarray(v) for k, v in inputs.items()}
    c = np.ascontiguousarray
    lut4 = g["L1_ffn_lut4"].reshape(KT, 4, POS, GO, NIB).transpose(0, 2, 3, 1, 4)
    lut8 = g["L1_ffn_lut8"].reshape(KT, 4, POS, GO, NIB, NIB).transpose(0, 2, 3, 1, 4, 5)
    bd4 = np.zeros((KT, POS, GO, NIB, 4, POS, GO), np.float32)
    bd8 = np.zeros((KT, POS, GO, NIB, 4, GO, NIB), np.float32)
    for f in range(GO):
        bd8[:, :, f, :, :, f, :] = lut8[:, :, f].transpose(0, 1, 4, 2, 3)
        for pos in range(POS):
            bd4[:, pos, f, :, :, pos, f] = lut4[:, pos, f].transpose(0, 2, 1)
    tiles = lambda b: c(b[:2 * DIM].reshape(QKT, P).T)
    bqk1 = np.concatenate([g["L1_attn_bq"], g["L1_attn_bk"]])
    arrays = {
        "x": g["L0_attn_x"].reshape(TOK, DIM),
        "qkvw": g["L0_attn_attn_qkvw"],
        "bqk0": tiles(g["L0_attn_attn_qkvb"]),
        "bv0": c(g["L0_attn_attn_qkvb"][2 * DIM:]),
        "ow0": g["L0_attn_attn_ow"],
        "ob0": g["L0_attn_attn_ob"],
        "wbase": c(g["L0_ffn_W_base"].T),
        "bbase": g["L0_ffn_b_base"],
        "wrout": c(g["L0_ffn_W_router"].T),
        "brout": g["L0_ffn_b_router"],
        "lora_a": c(g["L0_ffn_lora_A"].transpose(1, 0, 2).reshape(DIM, EXPERTS * RANK)),
        "lora_b": g["L0_ffn_lora_B"].reshape(EXPERTS * RANK, DIM),
        "wq1": c(g["L1_attn_Wq"].T),
        "wk1": c(g["L1_attn_Wk"].T),
        "wv1": c(g["L1_attn_Wv"].T),
        "bqk1": tiles(bqk1),
        "bv1": g["L1_attn_bv"],
        "ow1": c(g["L1_attn_Wo"].T),
        "ob1": g["L1_attn_bo"],
        "qweight": c(g["L1_ffn_qweight"].transpose(1, 0, 2)),
        "bd4": bd4.reshape(KT * POS, P, 4, 32),
        "bd8": bd8.reshape(KT * POS, P, 4, P),
        "bffn": g["L1_ffn_bias"],
        "consts": constants(),
        "shifts": np.arange(BITS, dtype=np.int32),
    }
    nc = _bacc.Bacc("TRN2", target_bir_lowering=False, num_devices=1)
    args = [nc.dram_tensor(f"in_{n}", a.shape, mybir.dt.from_np(a.dtype), kind="ExternalInput").ap()
            for n, a in arrays.items()]
    args.append(nc.dram_tensor("out_0", (TOK, DIM), F32, kind="ExternalOutput").ap())
    program(nc, *args)
    r = _run(nc, [{f"in_{n}": c(a) for n, a in arrays.items()}], core_ids=[0])
    return r.results[0]["out_0"].reshape(BATCH, SEQ, DIM)
```

```python
from contextlib import ExitStack

import numpy as np

import concourse.bass as bass
from concourse import mybir

F32 = mybir.dt.float32
BF16 = mybir.dt.bfloat16
I32 = mybir.dt.int32
ALU = mybir.AluOpType
ACT = mybir.ActivationFunctionType
AX = mybir.AxisListType.X

P = 128
BATCH, SEQ, DIM = 2, 1024, 512
HEADS, HD = 32, 16
TOK = BATCH * SEQ
KT = DIM // P
CHUNK = 512
TT = CHUNK // P
NCH = SEQ // CHUNK
CHUNKS = BATCH * NCH
QUAD = 4
QUADS = HEADS // QUAD
STEPS = BATCH * QUADS
VW = 2 * HD
PARTS = 3
Q_ROWS = (0, 0, 0, 1, 1, 2)
K_ROWS = (0, 1, 2, 0, 1, 0)
SROWS = len(Q_ROWS) * HD
BROWS = SROWS + 2
QT = SEQ // P
QHS = SEQ // CHUNK
EXPERTS, RANK = 8, 16
NSTAGE = 3
QKT = 2 * DIM // P
PLANES, WORDS, BITS = 8, 16, 32
GO = 8
NIB = 16
POS = 4
LOADS = len(Q_ROWS) + len(K_ROWS) + 1
DMA = 16
EPS = 1e-5
SCALE = 1.0 / float(np.sqrt(HD))
MASKED = -1e38
NORM_T = 64.0

C_ID = 0
C_SEL = C_ID + P
C_KCOL = C_SEL + POS * 32
C_KARR = C_KCOL + 1
C_UP = C_KARR + EXPERTS
C_LO = C_UP + P
C_ALL = C_LO + P


def constants():
    c = np.zeros((P, C_ALL), np.float32)
    p = np.arange(P)
    c[:, C_ID:C_ID + P] = np.eye(P)
    for pos in range(POS):
        c[p, C_SEL + 32 * pos + GO * pos + p // NIB] = 1.0
    c[:, C_KCOL] = p % NIB
    c[:, C_KARR:C_KARR + EXPERTS] = np.arange(1, EXPERTS + 1)
    c[:, C_UP:C_UP + P] = np.where(p[None, :] > p[:, None], MASKED, 0.0)
    c[:, C_LO:C_LO + P] = np.where(p[:, None] > p[None, :], MASKED, 0.0)
    return c


def a_units(causal):
    units = []
    for h in range(QUAD):
        for qt in range(QT):
            n = (qt + 1) * P if causal else SEQ
            for half in range((n + CHUNK - 1) // CHUNK):
                units.append((h, qt, half, n <= CHUNK, half * CHUNK, min(CHUNK, n - half * CHUNK)))
    return units


def b_groups(causal):
    groups = []
    for qh in range(QHS):
        kts = min(QT, (qh + 1) * CHUNK // P) if causal else QT
        for kt in range(kts):
            off = max(0, kt * P - qh * CHUNK) if causal else 0
            groups.append((qh, kt, off, kt == kts - 1))
    return groups


UNITS = [a_units(False), a_units(True)]
GROUPS = [b_groups(False), b_groups(True)]
RING = 3
LAG = 1
HEAD_TILES = 2 * QT
FIRST = 3
LEAD = [16, 12]


class Then:
    def __init__(self, eng, sem, base, i, per):
        self.eng, self.sem, self.start, self.n, self.per = eng, sem, per * i + base, 0, per

    def __call__(self, ins, wait=True):
        self.n += 1
        ins.then_inc(self.sem, 1)
        if wait:
            self.eng.wait_ge(self.sem, self.start + self.n)


CHAIN = [62, 20]
ONE = 2
PROJECT = 2
LN_STATS = 4
LN_SQRT = 6


def program(nc, x, qkvw, bqk0, bv0, ow0, ob0, wbase, bbase, wrout, brout, lora_a, lora_b,
            wq1, wk1, wv1, bqk1, bv1, ow1, ob1, qweight, bd4, bd8, bffn, consts, shifts, out):
    def dram(name, shape, dt=F32):
        return nc.dram_tensor(name, shape, dt).ap()

    qp = [dram(f"q_parts{l}", [PARTS, BATCH * DIM, SEQ], BF16) for l in range(2)]
    kp = [dram(f"k_parts{l}", [PARTS, BATCH * DIM, SEQ], BF16) for l in range(2)]
    vp = [dram(f"v_ones{l}", [STEPS, SEQ, QUAD * VW]) for l in range(2)]
    ctxd = [dram(f"ctx{l}", [BATCH * DIM, SEQ]) for l in range(2)]
    dend = [dram(f"den{l}", [BATCH * HEADS, SEQ]) for l in range(2)]
    rdend = [dram(f"rden{l}", [BATCH * HEADS, SEQ]) for l in range(2)]
    resd = [dram(f"res{l}", [TOK, DIM]) for l in range(2)]
    coded = dram("code_halves", [KT, POS, GO, 4, 2, DIM], BF16)

    with ExitStack() as ctx:
        def sb(name, shape, dt=F32):
            return ctx.enter_context(nc.sbuf_tensor(name, shape, dt))

        def sem(name):
            return ctx.enter_context(nc.semaphore(name))

        def sems(prefix, names):
            return {n: sem(f"{prefix}_{n}") for n in names.split()}

        cst = sb("cst", [P, C_ALL])
        shf = sb("shf", [P, BITS], I32)
        ident = cst[:, C_ID:C_ID + P]
        kcol = cst[:, C_KCOL:C_KCOL + 1]
        karr = cst[:, C_KARR:C_KARR + EXPERTS]
        idb = sb("idb", [P, P], BF16)
        upb = sb("upb", [P, P], BF16)
        lob = sb("lob", [P, P], BF16)
        wqkv = sb("wqkv", [P, KT, 3 * DIM])
        wo = sb("wo", [P, 2, KT, DIM])
        wrl = sb("wrl", [P, KT, EXPERTS * RANK + EXPERTS])
        lb = sb("lb", [P, DIM])
        w4 = sb("w4", [P, KT, DIM])
        w8 = sb("w8", [P, KT, DIM])
        wff = w4
        bqk = sb("bqk", [P, 2, QKT])
        bv = sb("bv", [P, 2, DIM])
        rb = sb("rb", [P, 2, DIM])
        rbp = sb("rbp", [P, 2, 2, DIM])
        brt = sb("brt", [P, EXPERTS])
        qwt = sb("qwt", [P, KT, PLANES, WORDS], I32)

        STAGE = QUAD * SEQ + QT * QUAD * VW
        FRONT_WORDS = 20480
        arena = sb("arena", [P, FRONT_WORDS + STAGE])

        class Layout:
            def __init__(self, at, end=FRONT_WORDS, on=arena):
                self.at, self.end, self.on = at, end, on

            def take(self, n, dt=F32):
                words = n if dt != BF16 else n // 2
                a = self.on[:, self.at:self.at + words]
                self.at += words
                assert self.at <= self.end, self.at
                return a if dt == F32 else a.bitcast(dt)

        def stage(at, on=arena):
            a = Layout(at, FRONT_WORDS + STAGE, on)
            q, k = (a.take(QUAD * SEQ, BF16).rearrange("p (h t) -> p h t", h=QUAD) for _ in range(2))
            return q, k, a.take(QT * QUAD * VW).rearrange("p (k w) -> p k w", k=QT)

        flat = wqkv[:, :, :].rearrange("p k n -> p (k n)")
        qst, kst, vst = zip(*(zip(stage(FRONT_WORDS), second, stage(STAGE)) for second in (stage(0), stage(0, flat))))
        pr = Layout(2 * STAGE).take(2 * QUAD * CHUNK).rearrange("p (a h t) -> p a h t", a=2, h=QUAD)

        EARLY = 2 * STAGE + 2 * QUAD * CHUNK

        def chunk_place(at):
            fr = Layout(at)
            return (fr.take(KT * CHUNK).rearrange("p (k t) -> p k t", k=KT),
                    fr.take(KT * CHUNK).rearrange("p (k t) -> p k t", k=KT),
                    fr.take(TT * DIM).rearrange("p (t d) -> p t d", t=TT))

        cxn, rdr, xb = zip(chunk_place(EARLY), chunk_place(0))
        fr = Layout(0, EARLY)
        xn = fr.take(TT * DIM).rearrange("p (t d) -> p t d", t=TT)
        xr = fr.take(TT * DIM).rearrange("p (t d) -> p t d", t=TT)
        xnt = fr.take(KT * CHUNK).rearrange("p (k t) -> p k t", k=KT)
        qf = fr.take(2 * CHUNK).rearrange("p (a t) -> p a t", a=2)
        qr = fr.take(2 * CHUNK).rearrange("p (a t) -> p a t", a=2)
        qs = fr.take(2 * PARTS * CHUNK, BF16).rearrange("p (a c t) -> p a c t", a=2, c=PARTS)
        vt = fr.take(2 * HEADS * VW).rearrange("p (a h w) -> p a h w", a=2, h=HEADS)
        rt = fr.take(2 * DIM).rearrange("p (a d) -> p a d", a=2)
        f0 = Layout(EARLY, EARLY + 2 * KT * CHUNK)
        bits, bits2, half0, half1 = (f0.take(WORDS * BITS, I32).bitcast(I32) for _ in range(4))
        half = (half0, half1)
        codeb = f0.take(2 * DIM, BF16).rearrange("p (c i) -> p c i", c=2)
        f0 = Layout(fr.at, EARLY)
        hs_words, hw_words = (f0.take(TT * EXPERTS * RANK) for _ in range(2))
        hs, hw = (a.rearrange("p (t e r) -> p t e r", t=TT, e=EXPERTS) for a in (hs_words, hw_words))
        hwt = f0.take(TT * P).rearrange("p (t q) -> p t q", t=TT)
        f1 = Layout(fr.at, EARLY)
        ysel = f1.take(2 * DIM).rearrange("p (a d) -> p a d", a=2)
        junk = f1.take(DIM)

        REP = 4 * 2 * DIM // 2
        codes = lambda words: words.bitcast(BF16).rearrange("p (j c i) -> p j c i", j=4, c=2)
        tabs = lambda words: words.rearrange("p (a j m) -> p a j m", a=POS, j=4)
        dq = Layout(STAGE, EARLY)
        msk = dq.take(2 * POS * DIM).rearrange("p (a j i) -> p a j i", a=2, j=POS)
        rep = [codes(flat[:, n * REP:(n + 1) * REP]) for n in range(3)] + [codes(dq.take(REP))]
        bd4s = tabs(hs_words)
        wrow = Layout(EARLY - 2 * DIM, EARLY).take(2 * DIM).rearrange("p (a i) -> p a i", a=2)
        dq = Layout(EARLY)
        oh = dq.take(2 * POS * DIM).rearrange("p (a j i) -> p a j i", a=2, j=POS)
        bd8s = tabs(dq.take(POS * 4 * P))

        eps_col = sb("eps_col", [P, 1])
        stats = sb("stats", [P, TT, 6])
        mv = sb("mv", [P, 4, TT])
        std = sb("std", [P, TT])
        rstd = sb("rstd", [P, TT])
        lg = sb("lg", [P, TT, EXPERTS])
        sm = sb("sm", [P, 8, TT, EXPERTS])
        sc = sb("sc", [P, 4, TT])
        nrm = sb("nrm", [P, 4, TT])
        mx = sb("mx", [P, 2, QUAD, QT])
        mmx = sb("mmx", [P, QUAD, QT])
        mrow = sb("mrow", [QUAD * QT, 2, P], BF16)
        cx = sb("cx", [P, 2, CHUNK])
        DW = QUAD * SEQ // P
        dni = sb("dni", [P, DW])
        dno = sb("dno", [P, DW])

        bank = [ctx.enter_context(nc.psum_tensor(f"bank{i}", [P, CHUNK], F32)) for i in range(4)]
        pair = [ctx.enter_context(nc.psum_tensor(f"pair{i}", [P, 2, CHUNK], F32)) for i in range(2)]
        banks = [b[:, :] for b in bank] + [pair[i // 2][:, i % 2, :] for i in range(4)]

        s_x0 = sem("s_x0")
        s_cst = sem("s_cst")
        s_wrl = sem("s_wrl")
        s_wqk = sem("s_wqk")
        s_wv = sem("s_wv")
        s_wy = sem("s_wy")
        s_wo = sem("s_wo")
        s_w1 = sem("s_w1")
        s_rb = sem("s_rb")
        s_prep = sem("s_prep")
        s_ones = sem("s_ones")
        step = sem("dve_step")
        D = sems("dq", "qw code code_out in0 in1 in2 in3 oh tab wl msk wsum wrow wt wt_used")
        D["in"] = [D[f"in{n}"] for n in range(POS)]
        FRONT = "x_in0 stat sqrt xn xr tp xnt qk qk_f qk_r qk_3 qk_out0 qk_out1 v v_used v_out0 v_out1 y y_used y_out0 y_out1"
        MIX = " ctx_in0 ctx_n x1 x_ready"
        F = [sems("f0", FRONT + " h hl_used hw hwt_ps hwt"), sems("f1", FRONT + MIX + " y_sel sq nsqrt mask"),
             sems("f2", "x_in0 x_in1 x_in2 x_in3 ctx_in1 ctx_in2 ctx_in3 out0 out1" + MIX)]
        AN = ("a_ready a_used mm mrow mload s_ready e_done pv_done cx cx_free cx_out0 cx_out1 den rden rden_out "
              "load0 load1 load2")
        A = [sems(f"a{l}", AN) for l in range(2)]
        SOFT = ("in", *(f"{n}_in{i}" for n in ("x", "ctx") for i in range(CHUNKS)), "cx_out0", "cx_out1", "den", "rden_out")
        counted = [s for group in (D, *F, *A) for n, s in group.items() if n not in SOFT]

        def mix_bank(l, i, t, first=False):
            return 1 + t % 2 if first else 2 + t % 2 if l < 2 else TT * (i % 2) + t

        place = lambda l, i: i % 2 if l == 2 else 0
        chunk_sem = lambda l, n, i: F[l][f"{n}_in{i if l == 2 else 0}"]
        turn = lambda l, i: 0 if l == 2 else i

        def context_loads(eng, l, i):
            S, pl, a = F[l], l - 1, place(l, i)
            b, c = i // NCH, i % NCH
            cols = slice(c * CHUNK, (c + 1) * CHUNK)
            eng.wait_ge(A[pl]["rden_out"], DMA * QUADS * (b + 1))
            if i > a:
                eng.wait_ge(S["x1"], ONE + TT * (i - a if l < 2 else i - 1))
            src = ctxd[pl][b * DIM:(b + 1) * DIM, cols]
            eng.dma_start(cxn[a], src.rearrange("(k p) t -> p k t", p=P)).then_inc(chunk_sem(l, "ctx", i), DMA)
            for k in range(KT):
                h = P // HD
                src = rdend[pl][b * HEADS + k * h:b * HEADS + (k + 1) * h, cols]
                eng.dma_start(rdr[a][:, k], src.unsqueeze(1).to_broadcast([h, HD, CHUNK]))\
                   .then_inc(chunk_sem(l, "ctx", i), DMA)

        def row_loads(eng, l, i):
            S, a = F[l], place(l, i)
            if l == 2 and i > 1:
                eng.wait_ge(S[f"out{a}"], ONE + DMA * TT * (i // 2))
            elif l < 2:
                eng.wait_ge(S["xn"], ONE + TT * i)
            src = (x if l == 0 else resd[l - 1])[i * CHUNK:(i + 1) * CHUNK, :]
            eng.dma_start(xb[a], src.rearrange("(t p) d -> p t d", p=P)).then_inc(chunk_sem(l, "x", i), DMA)

        def table_load(eng, ot, pos):
            rows = coded[bass.ds(ot, 1), pos].rearrange("k o j c i -> (k o) (j c i)")
            eng.dma_start(rep[pos].rearrange("p j c i -> p (j c i)"),
                          rows.unsqueeze(1).to_broadcast([GO, NIB, 4 * 2 * DIM])).then_inc(D["in"][pos], DMA)
            for dst, src in ((bd8s, bd8), (bd4s, bd4)):
                eng.dma_start(dst[:, pos], src[bass.ds(ot * POS + pos, 1)].rearrange("o p j m -> p (o j) m"))\
                   .then_inc(D["in"][pos], DMA)

        block = ctx.enter_context(nc.Block())

        @block.sync
        def _(sp):
            sp.dma_start(xb[0], x[0:CHUNK, :].rearrange("(t p) d -> p t d", p=P)).then_inc(s_x0, DMA)
            sp.dma_start(cst[:, :], consts).then_inc(s_cst, DMA)
            sp.dma_start(shf[:, :], shifts.partition_broadcast(P)).then_inc(s_cst, DMA)
            sp.wait_ge(s_x0, DMA)
            sp.dma_start(qwt[:, :, :, :], qweight.rearrange("(k p) e w -> p k e w", p=P)).then_inc(D["qw"], DMA)
            sp.wait_ge(D["qw"], ONE + DMA)
            sp.dma_start(wo[:, 0], ow0.rearrange("(k p) n -> p k n", p=P)).then_inc(s_wo, DMA)
            sp.dma_start(wo[:, 1], ow1.rearrange("(k p) n -> p k n", p=P)).then_inc(s_wo, DMA)

            def chunk_stores(l, i, b, c, last=False):
                S = F[l]
                for ot in range(QKT):
                    sp.wait_ge(S["qk_3"], ONE + QKT * i + ot + 1)
                    parts = (qp if ot < KT else kp)[l]
                    dst = parts[:, bass.ds(b * DIM + ot % KT * P, P), bass.ds(c * CHUNK, CHUNK)]
                    sp.dma_start(dst.rearrange("c p t -> p c t"), qs[:, ot % 2]).then_inc(S[f"qk_out{ot % 2}"], DMA)
                if l == 0:
                    sp.wait_ge(D["code"], ONE + 2 * (i + 1))
                    for j in range(4):
                        dst = coded[bass.ds(i, 1), :, :, j].rearrange("k a o c i -> (k a o) c i")
                        sp.dma_start(dst, codeb[32 * j:32 * (j + 1)]).then_inc(D["code_out"], DMA)
                for t in range(TT):
                    sp.wait_ge(S["v_used"], ONE + TT * i + t + 1)
                    dst = vp[l][bass.ds(b * QUADS, QUADS), bass.ds(c * CHUNK + t * P, P), :]
                    sp.dma_start(dst.rearrange("s p w -> p s w"),
                                 vt[:, t % 2].rearrange("p (s h) w -> p s (h w)", s=QUADS))\
                      .then_inc(S[f"v_out{t % 2}"], DMA)
                if l and last:
                    sp.wait_ge(S["v"], ONE + TT * CHUNKS)
                    load(l, 1, 1)
                for t in range(TT):
                    sp.wait_ge(S["y_used"], ONE + TT * i + t + 1)
                    sp.dma_start(resd[l][bass.ds(i * CHUNK + t * P, P), :], rt[:, t % 2])\
                      .then_inc(S[f"y_out{t % 2}"], DMA)

            def stored(l, n):
                S = F[l]
                for q in ("qk_out0", "qk_out1"):
                    sp.wait_ge(S[q], ONE + DMA * n * QKT // 2)
                for q in ("v_out0", "v_out1", "y_out0", "y_out1"):
                    sp.wait_ge(S[q], ONE + DMA * n * TT // 2)

            def load(l, it, st):
                s = A[l][f"load{st}"]
                for parts, stage, rows in ((qp[l], qst, Q_ROWS), (kp[l], kst, K_ROWS)):
                    for n, part in enumerate(rows):
                        src = parts[part, bass.ds(it * QUAD * HD, QUAD * HD), :]
                        sp.dma_start(stage[l][st][n * HD:(n + 1) * HD], src.rearrange("(h d) t -> d h t", d=HD))\
                          .then_inc(s, DMA)
                src = vp[l][bass.ds(it, 1)].rearrange("o (k p) w -> p (o k) w", p=P)
                sp.dma_start(vst[l][st], src).then_inc(s, DMA)

            def front_stores(l):
                sp.wait_ge(s_ones, 1 + 4 * l)
                with sp.Fori(0, NCH) as c:
                    chunk_stores(l, c, 0, c)
                stored(l, NCH)
                if l:
                    sp.wait_ge(A[0]["pv_done"], ONE + len(GROUPS[0]) * STEPS)
                load(l, 0, 0)
                for c in range(NCH):
                    chunk_stores(l, NCH + c, 1, c, c == NCH - 1)
                if l == 0:
                    stored(l, CHUNKS)

            def table_loads():
                table_load(sp, 0, POS - 1)
                load(0, 1, 1)
                with sp.Fori(1, KT) as ot:
                    for pos in range(POS):
                        sp.wait_ge(D["wsum"], ONE + POS * (ot - 1) + pos + 1)
                        table_load(sp, ot, pos)

            def attention_loads(l):
                S, nb = A[l], len(GROUPS[l])

                def max_rows(it, st):
                    sp.wait_ge(S["mrow"], ONE + it + 1)
                    for n in range(2):
                        r = SROWS + n
                        sp.dma_start(qst[l][st][r:r + 1].rearrange("o h (q t) -> o (h q) t", t=P), mrow[:, n, :])\
                          .then_inc(S["mload"], DMA)

                max_rows(0, 0)
                if l == 0:
                    sp.wait_ge(D["wt_used"], ONE + 2 * KT * KT)
                else:
                    stored(l, CHUNKS)
                load(l, 2, 2)
                rounds = (STEPS - 1) // NSTAGE

                def after(it, r, more):
                    max_rows(it + 1, (r + 1) % NSTAGE)
                    if more:
                        sp.wait_ge(S["pv_done"], ONE + nb * (it + 1))
                        load(l, it + NSTAGE, r)

                with sp.Fori(0, rounds - 1) as u:
                    for r in range(NSTAGE):
                        after(u * NSTAGE + r, r, True)
                for it in range(NSTAGE * (rounds - 1), STEPS - 1):
                    after(it, it % NSTAGE, it + NSTAGE < STEPS)

            front_stores(0)
            table_loads()
            attention_loads(0)
            front_stores(1)
            attention_loads(1)
            S = F[2]
            with sp.Fori(0, BATCH) as b:
                for c in range(NCH):
                    for t in range(TT):
                        sp.wait_ge(S["x_ready"], ONE + TT * (NCH * b + c) + t + 1)
                        sp.dma_start(out[bass.ds(b * SEQ + c * CHUNK + t * P, P), :], xb[c][:, t])\
                          .then_inc(S[f"out{c}"], DMA)
            for c in range(NCH):
                sp.wait_ge(S[f"out{c}"], ONE + DMA * TT * BATCH)

        @block.gpsimd
        def _(pool):
            for n, a in enumerate((ob0, bbase, ob1, bffn)):
                pool.dma_start(rbp[:, n // 2, n % 2], a.partition_broadcast(P)).then_inc(s_rb, DMA)
            pool.memset(vt[:, :, :, HD:], 1.0).then_inc(s_ones, 1)

            def residual(l, i):
                S = F[l]
                if l == 0:
                    pool.wait_ge(S["x_in0"] if i else s_x0, DMA * max(i, 1))
                else:
                    pool.wait_ge(S["x_ready"], ONE + TT * (i + 1))
                pool.wait_ge(S["y_used"], ONE + TT * i)
                for t in range(TT):
                    pool.tensor_tensor(xr[:, t], xb[0][:, t], rb[:, l], ALU.add).then_inc(S["xr"], 1)
                pool.wait_ge(S["xr"], ONE + TT * (i + 1))

            def front(l):
                for i in range(CHUNKS):
                    if i + 1 < CHUNKS and l:
                        context_loads(pool, l, i + 1)
                    residual(l, i)
                    if i + 1 < CHUNKS:
                        row_loads(pool, l, i + 1)

            def stage_ones(l, st):
                pool.memset(kst[l][st][SROWS:BROWS], 1.0).then_inc(s_ones, 1)

            def stored(l):
                S = F[l]
                for n in ("qk_out0", "qk_out1"):
                    pool.wait_ge(S[n], ONE + DMA * CHUNKS * QKT // 2)
                for n in ("v_out0", "v_out1", "y_out0", "y_out1"):
                    pool.wait_ge(S[n], ONE + DMA * CHUNKS * TT // 2)

            def attention(l):
                S = A[l]

                def context_store(it, qh):
                    pool.wait_ge(S["cx"], ONE + 2 * it + qh + 1)
                    cols = slice(qh * CHUNK, (qh + 1) * CHUNK)
                    for j in range(QUAD):
                        pool.dma_start(ctxd[l][bass.ds(it * QUAD * HD + j * HD, HD), cols],
                                       cx[32 * j:32 * j + HD, qh]).then_inc(S[f"cx_out{qh}"], DMA)
                    pool.dma_start(dend[l][bass.ds(it * QUAD, QUAD), cols], cx[HD:P:32, qh])\
                        .then_inc(S[f"cx_out{qh}"], DMA)

                dense = lambda d, it: d[bass.ds(it * QUAD, QUAD), :].rearrange("r (a t) -> (r a) t", t=DW)

                def reciprocal_store(it):
                    pool.wait_ge(S["rden"], ONE + it + 1)
                    pool.dma_start(dense(rdend[l], it), dno[:, :]).then_inc(S["rden_out"], DMA)

                def denominators(it):
                    for qh in range(QHS):
                        pool.wait_ge(S[f"cx_out{qh}"], 5 * DMA * (it + 1))
                    pool.sem_inc(S["cx_free"], 1)
                    if type(it) is not int or it:
                        reciprocal_store(it - 1)
                    pool.dma_start(dni[:, :], dense(dend[l], it)).then_inc(S["den"], DMA)

                def one(it):
                    for qh in range(QHS):
                        context_store(it, qh)
                    denominators(it)

                one(0)
                with pool.Fori(1, QUADS + 1) as it:
                    one(it)
                context_loads(pool, l + 1, 0)
                row_loads(pool, l + 1, 0)
                with pool.Fori(QUADS + 1, STEPS - 1) as it:
                    one(it)
                if l:
                    pool.wait_ge(S["pv_done"], ONE + len(GROUPS[l]) * (STEPS - 1))
                    context_loads(pool, l + 1, 1)
                    row_loads(pool, l + 1, 1)
                one(STEPS - 1)
                reciprocal_store(STEPS - 1)

            pool.wait_ge(s_prep, 6)
            front(0)
            stage_ones(0, 0)
            stored(0)
            stage_ones(0, 1)
            pool.wait_ge(D["wt_used"], ONE + 2 * KT * KT)
            stage_ones(0, 2)
            w = lambda a: a.rearrange("(k p) n -> p k n", p=P)
            for n, a in enumerate((wq1, wk1, wv1)):
                pool.dma_start(wqkv[:, :, n * DIM:(n + 1) * DIM], w(a)).then_inc(s_w1, DMA)
            attention(0)
            pool.wait_ge(A[0]["pv_done"], ONE + len(GROUPS[0]) * STEPS)
            pool.memset(vt[:, :, :, HD:], 1.0).then_inc(s_ones, 1)
            front(1)
            pool.wait_ge(F[1]["v"], ONE + TT * CHUNKS)
            stage_ones(1, 1)
            stored(1)
            stage_ones(1, 2)
            attention(1)

        @block.scalar
        def _(act):
            copy = lambda o, i: act.activation(o, i, ACT.Copy)
            w = lambda a: a.rearrange("(k p) n -> p k n", p=P)
            ER = EXPERTS * RANK
            for n, (s, dst, src) in enumerate((
                    (s_wrl, wrl[:, :, 0:ER], w(lora_a)), (s_wrl, wrl[:, :, ER:], w(wrout)),
                    (s_wrl, brt[:, :], brout.partition_broadcast(P)),
                    (s_wqk, bqk[:, 0], bqk0), (s_wqk, bqk[:, 1], bqk1),
                    (s_wqk, wqkv[:, :, 0:2 * DIM], w(qkvw)[:, :, 0:2 * DIM]),
                    (s_wv, wqkv[:, :, 2 * DIM:], w(qkvw)[:, :, 2 * DIM:]),
                    (s_wv, bv[:, 0], bv0.partition_broadcast(P)),
                    (s_wv, bv[:, 1], bv1.partition_broadcast(P)),
                    (s_wy, wff[:, :, :], w(wbase)), (s_wy, lb[:, :], lora_b))):
                if n == 5:
                    act.wait_ge(s_x0, DMA)
                act.dma_start(dst, src).then_inc(s, DMA)
            for s in counted[::2]:
                act.sem_inc(s, ONE)
            act.wait_ge(s_cst, 2 * DMA)
            for o, c in ((idb, C_ID), (upb, C_UP), (lob, C_LO)):
                copy(o[:, :], cst[:, c:c + P]).then_inc(s_prep, 1)

            def deviation(l, i):
                S = F[l]
                act.wait_ge(S["stat"], ONE + (TT + 1) * (i + 1))
                act.activation(std[:, :], mv[:, 1], ACT.Sqrt, bias=eps_col[:, :]).then_inc(S["sqrt"], 1)

            def front(l):
                S = F[l]
                if l == 0:
                    act.wait_ge(s_prep, 4)
                deviation(l, 0)
                if l == 0:
                    act.wait_ge(s_wqk, 3 * DMA)

                def chunk(i, more):
                    for t in range(TT):
                        act.wait_ge(S["tp"], ONE + TT * i + t + 1)
                        if t == 0:
                            act.wait_ge(S["y"], ONE + TT * i)
                        copy(xnt[:, :, t * P:(t + 1) * P], banks[t % 2].rearrange("p (k q) -> p k q", k=KT))\
                            .then_inc(S["xnt"], 1)
                    for ot in range(QKT):
                        n = QKT * i + ot
                        act.wait_ge(S["qk"], ONE + n + 1)
                        act.wait_ge(S["qk_r"], ONE + (QKT * i if ot < 2 else n - 1))
                        act.wait_ge(S[f"qk_out{ot % 2}"], ONE + DMA * (QKT // 2 * i + ot // 2))
                        src, b = banks[4 + ot % 2], bqk[:, l, ot:ot + 1]
                        act.activation(qf[:, ot % 2], src, ACT.Identity, bias=b).then_inc(S["qk_f"], 1)
                        act.activation(qs[:, ot % 2, 0], src, ACT.Identity, bias=b).then_inc(S["qk_f"], 1)
                        if l and ot == 1:
                            for t in range(TT):
                                act.wait_ge(S["xn"], ONE + TT * i + t + 1)
                                act.wait_ge(S["sq"], ONE + TT * i + t)
                                act.activation(junk, xn[:, t], ACT.Square, accum_out=nrm[:, 0, t:t + 1])\
                                    .then_inc(S["sq"], 1)
                        if ot == LN_STATS:
                            if l:
                                act.wait_ge(S["sq"], ONE + TT * (i + 1))
                                act.activation(nrm[:, 1], nrm[:, 0], ACT.Sqrt).then_inc(S["nsqrt"], 1)
                        if more and ot == LN_SQRT:
                            deviation(l, i + 1)
                        if l == 0 and ot == QKT - 2:
                            act.wait_ge(S["hwt_ps"], ONE + i + 1)
                            copy(hwt, banks[3].rearrange("p (t q) -> p t q", t=TT)).then_inc(S["hwt"], 1)
                    for t in range(TT if l else 0):
                        n = TT * i + t
                        act.wait_ge(S["mask"], ONE + 2 * (i + 1))
                        act.wait_ge(S["y"], ONE + n + 1)
                        act.wait_ge(S["y_used"], ONE + (TT * i if t < 2 else n - 1))
                        act.activation(ysel[:, t % 2], banks[6 if t % 2 == 0 else 2], ACT.Copy,
                                       scale=nrm[:, 3, t:t + 1]).then_inc(S["y_sel"], 1)

                with act.Fori(0, CHUNKS - 1) as i:
                    chunk(i, True)
                chunk(CHUNKS - 1, False)

            def tables():
                with act.Fori(0, KT) as ot:
                    for n in range(2):
                        act.wait_ge(D["wl"] if n == 0 else D["wsum"], ONE + POS * (ot + 1))
                        act.wait_ge(D["wt_used"], ONE + 2 * KT * ot)
                        copy(wrow[:, n], banks[4 + n]).then_inc(D["wrow"], 1)
                        for k in range(KT):
                            act.wait_ge(D["wt"], ONE + 2 * KT * ot + KT * n + k + 1)
                            copy((w4, w8)[n][:, k, bass.ds(ot * P, P)], banks[6 + k % 2][:, 0:P]).then_inc(D["wt_used"], 1)

            def attention(l):
                S, groups = A[l], GROUPS[l]
                nb = len(groups)

                ends = [n for n, q in enumerate(groups) if q[3]]

                def exponentials(it, g):
                    off = groups[g][2]
                    for p in range(2):
                        act.wait_ge(S["s_ready"], ONE + 2 * nb * it + 2 * g + p + 1)
                        if p == 0:
                            act.wait_ge(S["pv_done"], ONE + nb * it + g - 1)
                        act.activation(pr[:, g % 2, 2 * p:2 * p + 2, off:], pair[p][:, :, off:], ACT.Exp,
                                       scale=SCALE).then_inc(S["e_done"], 1)

                def evacuate(it, qh):
                    act.wait_ge(S["pv_done"], ONE + nb * it + ends[qh] + 1)
                    act.wait_ge(S["cx_free"], ONE + it)
                    copy(cx[:, qh], banks[RING]).then_inc(S["cx"], 1)

                def step_(it, more):
                    for g in range(1, nb):
                        exponentials(it, g)
                        if g == ends[0] + 1:
                            evacuate(it, 0)
                    if more:
                        exponentials(it + 1, 0)
                    evacuate(it, 1)

                exponentials(0, 0)
                with act.Fori(0, (STEPS - 1) // NSTAGE) as u:
                    for r in range(NSTAGE):
                        step_(u * NSTAGE + r, True)
                step_(STEPS - 1, False)

            front(0)
            act.wait_ge(D["code_out"], ONE + 4 * DMA * KT)
            act.wait_ge(F[0]["v"], ONE + TT * CHUNKS)
            act.wait_ge(F[0]["hw"], ONE + TT * CHUNKS)
            act.wait_ge(F[0]["xr"], ONE + TT * CHUNKS)
            for pos in range(POS - 1):
                table_load(act, 0, pos)
            tables()
            attention(0)
            front(1)
            attention(1)
            for i in range(NCH, CHUNKS):
                context_loads(act, 2, i)
                row_loads(act, 2, i)

        @block.vector
        def _(dve):
            before = [0]

            dve.memset(eps_col[:, :], EPS).then_inc(s_prep, 1)

            def look_ups():
                S = A[0]

                def one_hot(ot, pos):
                    a, r = pos % 2, POS * ot + pos
                    dve.wait_ge(D["in"][pos], ONE + 3 * DMA * (ot + 1))
                    dve.wait_ge(D["wl"], ONE + (r - 1 if pos else r))
                    dve.tensor_scalar(oh[:, a], rep[pos][:, :, 0], kcol, None, ALU.is_equal).then_inc(D["oh"], 1)

                def masks(ot, pos):
                    a, r = pos % 2, POS * ot + pos
                    dve.wait_ge(D["wsum"], ONE + (r - 1 if pos else r))
                    for j in range(4):
                        dve.wait_ge(D["tab"], ONE + 4 * r + j + 1)
                        dve.scalar_tensor_tensor(out=msk[:, a, j], in0=rep[pos][:, j, 1], scalar=kcol, in1=banks[j],
                                                 op0=ALU.is_equal, op1=ALU.mult).then_inc(D["msk"], 1)
                        k = POS * pos + j
                        if k == 0:
                            dve.wait_ge(S["mm"], ONE + ot)
                        dve.wait_ge(S["a_ready"], ONE + HEAD_TILES * ot + k + 1)
                        dve.reduce_max(mx[:, k % 2, 0, k // 2:k // 2 + 1], banks[6 + k % 2], AX)\
                           .then_inc(S["a_used"], 1)

                def tile(ot, more):
                    for pos in range(POS):
                        if pos + 1 < POS:
                            one_hot(ot, pos + 1)
                        masks(ot, pos)
                        if pos + 1 == POS and more:
                            one_hot(ot + 1, 0)
                    dve.wait_ge(S["a_used"], ONE + HEAD_TILES * (ot + 1))
                    dve.tensor_tensor(mmx[:, bass.ds(ot, 1)], mx[:, 0, 0:1], mx[:, 1, 0:1], ALU.max).then_inc(S["mm"], 1)

                dve.wait_ge(F[0]["y_used"], ONE + TT * CHUNKS)
                one_hot(0, 0)
                for n in ("qk_out0", "qk_out1"):
                    dve.wait_ge(F[0][n], ONE + DMA * CHUNKS * QKT // 2)
                for n in ("v_out0", "v_out1"):
                    dve.wait_ge(F[0][n], ONE + DMA * CHUNKS * TT // 2)
                with dve.Fori(0, KT - 1) as ot:
                    tile(ot, True)
                tile(KT - 1, False)

            def context(l, i, a=0):
                S = F[l]
                dve.wait_ge(chunk_sem(l, "ctx", i), DMA * (1 + KT) * (turn(l, i) + 1))
                dve.tensor_tensor(cxn[a], cxn[a], rdr[a], ALU.mult).then_inc(S["ctx_n"], 1)

            def mix(l, i, a=0, first=False, tiles=range(TT)):
                S = F[l]
                dve.wait_ge(chunk_sem(l, "x", i), DMA * (turn(l, i) + 1))
                for t in tiles:
                    dve.wait_ge(S["x1"], ONE + TT * i + t + 1)
                    dve.tensor_tensor(xb[a][:, t], banks[mix_bank(l, i, t, first)], xb[a][:, t], ALU.add).then_inc(S["x_ready"], 1)

            def sparsemax(then):
                srt, cum, kz, sup, sel, w = (sm[:, n] for n in range(6))
                k4 = karr.unsqueeze(1).to_broadcast([P, TT, EXPERTS])
                for t in range(TT):
                    then(dve.max(srt[:, t], lg[:, t]), wait=t == TT - 1)
                then(dve.tensor_copy(cum[:, :, 0:1], srt[:, :, 0:1]))
                for e in range(1, EXPERTS):
                    then(dve.tensor_tensor(cum[:, :, e:e + 1], cum[:, :, e - 1:e], srt[:, :, e:e + 1], ALU.add))
                then(dve.tensor_tensor(kz, srt, k4, ALU.mult))
                then(dve.tensor_scalar(kz, kz, 1.0, None, ALU.add))
                then(dve.tensor_tensor(sup, kz, cum, ALU.is_gt))
                then(dve.reduce_sum(sc[:, 0], sup, AX))
                kb = sc[:, 0].unsqueeze(2).to_broadcast([P, TT, EXPERTS])
                then(dve.tensor_tensor(sel, k4, kb, ALU.is_equal))
                then(dve.tensor_tensor(sel, sel, cum, ALU.mult))
                then(dve.reduce_sum(sc[:, 1], sel, AX))
                then(dve.tensor_scalar(sc[:, 1], sc[:, 1], -1.0, None, ALU.add))
                then(dve.reciprocal(sc[:, 2], sc[:, 0]))
                then(dve.tensor_tensor(sc[:, 3], sc[:, 1], sc[:, 2], ALU.mult))
                tb = sc[:, 3].unsqueeze(2).to_broadcast([P, TT, EXPERTS])
                then(dve.tensor_tensor(w, lg[:, :, :], tb, ALU.subtract))
                then(dve.tensor_scalar(w, w, 0.0, None, ALU.max))
                return w

            def statistics(l, i, then):
                S = F[l]
                if l:
                    dve.wait_ge(S["x_ready"], ONE + TT * (i + 1))
                elif type(i) is int:
                    dve.wait_ge(s_x0, DMA)
                else:
                    dve.wait_ge(S["x_in0"], DMA * i)
                for t in range(TT):
                    dve.bn_stats(stats[:, t], xb[0][:, t]).then_inc(S["stat"], 1)
                dve.wait_ge(S["stat"], ONE + (TT + 1) * i + TT)
                (em, es), (om, os_) = ((stats[:, :, n], stats[:, :, n + 1]) for n in (1, 4))
                mean, var, dif, dev = (mv[:, n] for n in range(4))
                then(dve.tensor_tensor(mean, em, om, ALU.add), wait=False)
                then(dve.tensor_tensor(dif, em, om, ALU.subtract), wait=False)
                then(dve.tensor_tensor(dev, es, os_, ALU.add))
                then(dve.tensor_scalar(mean, mean, 0.5, None, ALU.mult), wait=False)
                then(dve.tensor_tensor(dif, dif, dif, ALU.mult))
                then(dve.tensor_scalar(dif, dif, 0.25, None, ALU.mult), wait=False)
                then(dve.tensor_scalar(dev, dev, 1.0 / DIM, None, ALU.mult))
                dve.tensor_tensor(var, dif, dev, ALU.add).then_inc(S["stat"], 1)

            def normalise(l, i, then):
                S = F[l]
                dve.wait_ge(S["sqrt"], ONE + i + 1)
                then(dve.reciprocal(rstd[:, :], std[:, :]))
                dve.wait_ge(S["tp"], ONE + TT * i)
                if l:
                    dve.wait_ge(S["sq"], ONE + TT * i)
                for t in range(TT):
                    dve.tensor_scalar(xn[:, t], xb[0][:, t], mv[:, 0, t:t + 1], rstd[:, t:t + 1], ALU.subtract, ALU.mult)\
                       .then_inc(S["xn"], 1)

            def code_plane(i, e, then):
                c, s = e // 4, e % 4
                shape = [P, WORDS, BITS]
                v = lambda a: a.rearrange("p (w b) -> p w b", w=WORDS)
                if e == 0:
                    dve.wait_ge(D["code_out"], ONE + 4 * DMA * i)
                plane = qwt[:, bass.ds(i, 1), e, :].rearrange("p k w -> p (k w)")
                then(dve.tensor_tensor(v(bits), plane.unsqueeze(2).to_broadcast(shape),
                                       shf[:, :].unsqueeze(1).to_broadcast(shape), ALU.logical_shift_right))
                then(dve.tensor_scalar(half[c] if s == 0 else bits2, bits, 1, s, ALU.bitwise_and,
                                       ALU.logical_shift_left))
                if s:
                    then(dve.tensor_tensor(half[c], half[c], bits2, ALU.bitwise_or))
                if s == 3:
                    dve.tensor_copy(codeb[:, c], half[c]).then_inc(D["code"], 1)

            def tile_maximum(l, it, k, tile):
                h, qt, hf, only, _, n = UNITS[l][k]
                dve.wait_ge(A[l]["a_ready"], ONE + (len(UNITS[l]) + 1) * it + k + 1)
                o = mmx[:, h, qt:qt + 1] if only else mx[:, hf, h, qt:qt + 1]
                dve.reduce_max(o, tile[:, 0:n], AX).then_inc(A[l]["a_used"], 1)

            def opening(l):
                then = Then(dve, step, before[0], 0, 8)
                statistics(l, 0, then)
                normalise(l, 0, then)
                before[0] += then.n

            def front(l):
                S = F[l]
                per = CHAIN[l]
                if l == 0:
                    opening(l)
                    dve.wait_ge(s_rb, 4 * DMA)
                    for n in range(2):
                        dve.tensor_tensor(rb[:, n], rbp[:, n, 0], rbp[:, n, 1], ALU.add).then_inc(s_prep, 1)
                base = before[0]
                if l == 0:
                    dve.wait_ge(s_wrl, 3 * DMA)
                    dve.wait_ge(s_wv, 3 * DMA)
                    dve.wait_ge(s_cst, 2 * DMA)
                    dve.wait_ge(D["qw"], ONE + DMA)

                def chunk(i, more):
                    then = Then(dve, step, base, i, per)
                    beside = iter(range(len(UNITS[1])))

                    def first_maxima(n=FIRST):
                        if l and not more:
                            for _, k in zip(range(n), beside):
                                tile_maximum(1, 0, k, banks[k % 2])

                    if l == 0:
                        dve.wait_ge(S["h"], ONE + 2 * i + 2)
                        dve.tensor_tensor(lg[:, :, :], banks[3][:, 0:TT * EXPERTS].rearrange("p (t e) -> p t e", t=TT),
                                          brt[:, :].unsqueeze(1).to_broadcast([P, TT, EXPERTS]), ALU.add)\
                           .then_inc(S["hl_used"], 1)
                        dve.wait_ge(S["hl_used"], ONE + 2 * i + 1)
                        dve.tensor_copy(hs.rearrange("p t e r -> p (t e r)"), banks[2]).then_inc(S["hl_used"], 1)
                        w = sparsemax(then)
                        for t in range(TT):
                            dve.tensor_tensor(hw[:, t], hs[:, t], w[:, t].unsqueeze(2).to_broadcast([P, EXPERTS, RANK]),
                                              ALU.mult).then_inc(S["hw"], 1)
                    elif more:
                        context(l, i + 1)
                    for ot in range(QKT):
                        n = QKT * i + ot
                        a = ot % 2
                        first_maxima(FIRST if ot else FIRST + 1)
                        dve.wait_ge(S["qk_f"], ONE + 2 * (n + 1))
                        dve.tensor_tensor(qr[:, a], qf[:, a], qs[:, a, 0], ALU.subtract).then_inc(S["qk_r"], 1)
                        dve.wait_ge(S["qk_r"], ONE + n + 1)
                        then(dve.tensor_copy(qs[:, a, 1], qr[:, a]))
                        dve.tensor_tensor(qs[:, a, 2], qr[:, a], qs[:, a, 1], ALU.subtract).then_inc(S["qk_3"], 1)
                        if l == 0:
                            code_plane(i, ot, then)
                        if more:
                            if l and ot == PROJECT:
                                mix(l, i + 1)
                            if ot == LN_STATS:
                                statistics(l, i + 1, then)
                            if ot == LN_SQRT:
                                normalise(l, i + 1, then)
                        if l and ot == LN_STATS + 1:
                            dve.wait_ge(S["nsqrt"], ONE + i + 1)
                            dve.tensor_scalar(nrm[:, 2], nrm[:, 1], NORM_T, None, ALU.is_gt).then_inc(S["mask"], 1)
                            dve.tensor_scalar(nrm[:, 3], nrm[:, 1], NORM_T, None, ALU.is_le).then_inc(S["mask"], 1)
                    for t in range(TT):
                        n = TT * i + t
                        first_maxima(FIRST if t < TT - 1 else FIRST - 1)
                        dve.wait_ge(S["v"], ONE + n + 1)
                        dve.wait_ge(S[f"v_out{t % 2}"], ONE + DMA * (TT // 2 * i + t // 2))
                        h3 = lambda a: a.rearrange("p (h d) -> p h d", h=HEADS)
                        dve.tensor_tensor(vt[:, t % 2, :, 0:HD], h3(banks[6 + t % 2]), h3(bv[:, l]), ALU.add)\
                           .then_inc(S["v_used"], 1)
                    dve.wait_ge(S["xr"], ONE + TT * (i + 1))
                    for t in range(TT):
                        n = TT * i + t
                        first_maxima()
                        dve.wait_ge(S["y"], ONE + n + 1)
                        dve.wait_ge(S[f"y_out{t % 2}"], ONE + DMA * (TT // 2 * i + t // 2))
                        if l == 0:
                            dve.tensor_tensor(rt[:, t % 2], banks[6 + t % 2], xr[:, t], ALU.add).then_inc(S["y_used"], 1)
                        else:
                            dve.wait_ge(S["y_sel"], ONE + n + 1)
                            then(dve.scalar_tensor_tensor(out=ysel[:, t % 2], in0=banks[7 if t % 2 == 0 else 3],
                                                          scalar=nrm[:, 2, t:t + 1], in1=ysel[:, t % 2],
                                                          op0=ALU.mult, op1=ALU.add))
                            dve.tensor_tensor(rt[:, t % 2], ysel[:, t % 2], xr[:, t], ALU.add).then_inc(S["y_used"], 1)
                    assert then.n == (per if more else per - 8), then.n

                with dve.Fori(0, CHUNKS - 1) as i:
                    chunk(i, True)
                chunk(CHUNKS - 1, False)
                before[0] = base + per * CHUNKS - 8

            def attention(l):
                S, units = A[l], UNITS[l]
                na = len(units)
                base = before[0]

                def maxima(it):
                    for k in range(na):
                        tile_maximum(l, it, k, banks[k % RING])
                    join(it)
                    negate(it)

                def join(it):
                    dve.wait_ge(S["a_used"], ONE + na * (it + 1))
                    q0 = min(qt for _, qt, _, only, _, _ in units if not only)
                    dve.tensor_tensor(mmx[:, :, q0:], mx[:, 0, :, q0:], mx[:, 1, :, q0:], ALU.max).then_inc(S["mm"], 1)

                def negate(it):
                    dve.wait_ge(S["a_ready"], ONE + (na + 1) * (it + 1))
                    dve.wait_ge(S["mload"], ONE + 2 * DMA * it)
                    rows = banks[na % RING][0:QUAD * QT, 0:P]
                    dve.tensor_scalar(mrow[:, 0], rows, -1.0, None, ALU.mult).then_inc(step, 1)
                    dve.wait_ge(step, base + it + 1)
                    dve.scalar_tensor_tensor(out=mrow[:, 1], in0=rows, scalar=-1.0, in1=mrow[:, 0],
                                             op0=ALU.mult, op1=ALU.subtract).then_inc(S["mrow"], 1)

                def reciprocals(it):
                    dve.wait_ge(S["den"], DMA * (it + 1))
                    if type(it) is not int or it:
                        dve.wait_ge(S["rden_out"], DMA * it)
                    dve.reciprocal(dno[:, :], dni[:, :]).then_inc(S["rden"], 1)

                if l:
                    join(0)
                negate(0)
                maxima(1)
                maxima(2)
                reciprocals(0)
                with dve.Fori(3, STEPS) as it:
                    maxima(it)
                    reciprocals(it - 2)
                before[0] = base + STEPS
                context(l + 1, 0)
                reciprocals(STEPS - 2)
                mix(l + 1, 0, 0, True)
                if l:
                    context(l + 1, 1, 1)
                else:
                    opening(l + 1)
                reciprocals(STEPS - 1)

            front(0)
            look_ups()
            attention(0)
            front(1)
            attention(1)
            for i in range(1, CHUNKS):
                mix(2, i, i % 2, tiles=range(TT - 1))
                if i + 1 < CHUNKS:
                    context(2, i + 1, (i + 1) % 2)
                mix(2, i, i % 2, tiles=range(TT - 1, TT))

        @block.tensor
        def _(pe):
            def product(o, pairs, start=True, stop=True, between=None):
                for n, (a, b) in enumerate(pairs):
                    if n and between:
                        between()
                    last = pe.matmul(o, a, b, start=start and n == 0, stop=stop and n == len(pairs) - 1)
                return last

            def score_tile(l, st, k, o):
                h, qt, _, _, k0, n = UNITS[l][k]
                diagonal = l == 1 and k0 + n == (qt + 1) * P
                ins = pe.matmul(o[:, 0:n], qst[l][st][0:SROWS, h, qt * P:(qt + 1) * P],
                                kst[l][st][0:SROWS, h, k0:k0 + n], start=True, stop=not diagonal)
                if diagonal:
                    ins = pe.matmul(o[:, n - P:n], idb[:, :], upb[:, :], start=False, stop=True)
                ins.then_inc(A[l]["a_ready"], 1)

            for s in counted[1::2]:
                pe.sem_inc(s, ONE)

            def tables():
                def first_scores(ot, k):
                    S = A[0]
                    if k < 2:
                        pe.wait_ge(D["wt_used"], ONE + 2 * KT * ot)
                    else:
                        pe.wait_ge(S["a_used"], ONE + HEAD_TILES * ot + k - 1)
                    qt, k0, head = k // 2, k % 2 * CHUNK, bass.ds(ot, 1)
                    pe.matmul(banks[6 + k % 2], qst[0][0][0:SROWS, head, qt * P:(qt + 1) * P].rearrange("r o t -> r (o t)"),
                              kst[0][0][0:SROWS, head, k0:k0 + CHUNK].rearrange("r o t -> r (o t)"),
                              start=True, stop=True).then_inc(S["a_ready"], 1)

                def pick(ot, pos):
                    a, r = pos % 2, POS * ot + pos
                    pe.wait_ge(D["in"][pos], ONE + 3 * DMA * (ot + 1))
                    pe.wait_ge(D["oh"], ONE + r + 1)
                    for j in range(4):
                        pe.wait_ge(D["msk"], ONE + (4 * (r - 1) + j + 1 if pos else 4 * r))
                        product(banks[j], [(bd8s[:, pos, j], oh[:, a, j])]).then_inc(D["tab"], 1)
                        first_scores(ot, POS * pos + j)
                    if pos == 0:
                        pe.wait_ge(D["wrow"], ONE + 2 * ot)
                    for j in range(4):
                        last = product(banks[4][32 * j:32 * j + 32], [(bd4s[:, pos, j], oh[:, a, j])],
                                       start=pos == 0, stop=pos == POS - 1)
                    last.then_inc(D["wl"], 1)

                def add_up(ot, pos):
                    a, r = pos % 2, POS * ot + pos
                    for j in range(4):
                        pe.wait_ge(D["msk"], ONE + 4 * r + j + 1)
                        last = product(banks[5][32 * j:32 * j + 32],
                                       [(cst[:, C_SEL + 32 * pos:C_SEL + 32 * pos + 32], msk[:, a, j])],
                                       start=pos == 0, stop=pos == POS - 1)
                    last.then_inc(D["wsum"], 1)

                def turn(ot, n):
                    pe.wait_ge(D["wrow"], ONE + 2 * ot + n + 1)
                    if n == 0:
                        pe.wait_ge(A[0]["a_used"], ONE + HEAD_TILES * (ot + 1))
                    for k in range(KT):
                        m = KT * n + k
                        pe.wait_ge(D["wt_used"], ONE + 2 * KT * ot + (m - 1 if m >= 2 else 0))
                        pe.transpose(banks[6 + k % 2][:, 0:P], wrow[:, n, k * P:(k + 1) * P], ident)\
                          .then_inc(D["wt"], 1)

                with pe.Fori(0, KT) as ot:
                    for pos in range(POS):
                        pick(ot, pos)
                        if pos:
                            add_up(ot, pos - 1)
                    turn(ot, 0)
                    add_up(ot, POS - 1)
                    turn(ot, 1)

            def project_tile(l, i, t, first=False):
                S = F[l]
                n = TT * i + t
                if t == 0:
                    pe.wait_ge(S["ctx_n"], ONE + i + 1)
                if l == 2 and not first:
                    if i == CHUNKS - 1:
                        pe.wait_ge(S["x_ready"], ONE + TT * (i - 2) + t + 1)
                elif t >= 2:
                    pe.wait_ge(S["x_ready"], ONE + n - 1)
                elif not first:
                    pe.wait_ge(S["y_used"], ONE + TT * (i - 1))
                src = cxn[place(l, i)]
                product(banks[mix_bank(l, i, t, first)], [(src[:, k, t * P:(t + 1) * P], wo[:, l - 1, k]) for k in range(KT)])\
                    .then_inc(S["x1"], 1)

            def front(l):
                S = F[l]
                ER = EXPERTS * RANK

                def chunk(i, more):
                    beside = iter(range(len(UNITS[1])))

                    def first_scores():
                        for _, k in zip(range(1), beside):
                            if k == 0:
                                pe.wait_ge(A[1]["load0"], ONE + LOADS * DMA)
                            if k >= 2:
                                pe.wait_ge(A[1]["a_used"], ONE + k - 1)
                            score_tile(1, 0, k, banks[k % 2])

                    between = first_scores if l and not more else None
                    for t in range(TT):
                        n = TT * i + t
                        pe.wait_ge(S["xn"], ONE + n + 1)
                        pe.wait_ge(S["xnt"], ONE + (n - 1 if t >= 2 else TT * i))
                        for k in range(KT):
                            last = pe.transpose(banks[t % 2][:, k * P:(k + 1) * P], xn[:, t, k * P:(k + 1) * P], ident)
                        last.then_inc(S["tp"], 1)
                    pe.wait_ge(S["xnt"], ONE + TT * (i + 1))
                    tok = lambda k, t: xnt[:, k, t * P:(t + 1) * P]
                    if l == 0:
                        pe.wait_ge(s_wrl, 3 * DMA)
                        pe.wait_ge(S["hl_used"], ONE + 2 * i)
                        for t in range(TT):
                            last = product(banks[2][:, t * ER:(t + 1) * ER],
                                           [(tok(k, t), wrl[:, k, 0:ER]) for k in range(KT)])
                        last.then_inc(S["h"], 1)
                        pe.wait_ge(S["hwt"], ONE + i)
                        for t in range(TT):
                            last = product(banks[3][:, t * EXPERTS:(t + 1) * EXPERTS],
                                           [(tok(k, t), wrl[:, k, ER:]) for k in range(KT)])
                        last.then_inc(S["h"], 1)
                        pe.wait_ge(s_wqk, 3 * DMA)
                    for ot in range(QKT):
                        n = QKT * i + ot
                        pe.wait_ge(S["qk_f"], ONE + (2 * (n - 1) if ot >= 2 else 2 * QKT * i))
                        product(banks[4 + ot % 2], [(wqkv[:, k, ot * P:(ot + 1) * P], xnt[:, k]) for k in range(KT)],
                                between=between).then_inc(S["qk"], 1)
                        if l and more and ot == PROJECT:
                            for t in range(TT):
                                project_tile(l, i + 1, t)
                        if l == 0 and ot == LN_STATS:
                            pe.wait_ge(S["hw"], ONE + TT * (i + 1))
                            for t in range(TT):
                                last = pe.transpose(banks[3][:, t * P:(t + 1) * P],
                                                    hw[:, t].rearrange("p e r -> p (e r)"), ident)
                            last.then_inc(S["hwt_ps"], 1)
                    if l == 0:
                        pe.wait_ge(s_wv, 3 * DMA)
                    for t in range(TT):
                        n = TT * i + t
                        if t >= 2:
                            pe.wait_ge(S["v_used"], ONE + n - 1)
                        else:
                            pe.wait_ge(S["y_used"], ONE + TT * i)
                        product(banks[6 + t % 2], [(tok(k, t), wqkv[:, k, 2 * DIM:]) for k in range(KT)],
                                between=between).then_inc(S["v"], 1)
                    if l == 0:
                        pe.wait_ge(s_wy, 2 * DMA)
                    if l == 0:
                        pe.wait_ge(S["hwt"], ONE + i + 1)
                    for t in range(TT):
                        n = TT * i + t
                        if t >= 2:
                            pe.wait_ge(S["y_used"], ONE + n - 1)
                        else:
                            pe.wait_ge(S["v_used"], ONE + TT * i + (TT if l else t + 3))
                        if l == 0:
                            product(banks[6 + t % 2], [(tok(k, t), wff[:, k]) for k in range(KT)] + [(hwt[:, t], lb[:, :])])\
                                .then_inc(S["y"], 1)
                        else:
                            lo, hi = (6, 7) if t % 2 == 0 else (2, 3)
                            product(banks[lo], [(tok(k, t), w4[:, k]) for k in range(KT)], between=between)
                            product(banks[hi], [(tok(k, t), w8[:, k]) for k in range(KT)]).then_inc(S["y"], 1)

                with pe.Fori(0, CHUNKS - 1) as i:
                    chunk(i, True)
                chunk(CHUNKS - 1, False)

            def attention(l):
                S, units, groups = A[l], UNITS[l], GROUPS[l]
                na, nb, causal = len(units), len(groups), l == 1

                def ring_tile(it, st, k):
                    if k < RING:
                        pe.wait_ge(S["a_used"], ONE + na * it)
                        pe.wait_ge(S["mrow"], ONE + it)
                    else:
                        pe.wait_ge(S["a_used"], ONE + na * it + k - RING + 1)
                    score_tile(l, st, k, banks[k % RING])

                def maxima_rows(it):
                    pe.wait_ge(S["mm"], ONE + it + (1 if causal else QUAD))
                    pe.transpose(banks[na % RING][0:QUAD * QT, 0:P], mmx[:, :, :].rearrange("p h q -> p (h q)"), ident)\
                        .then_inc(S["a_ready"], 1)

                def transposed_scores(it, st, g, p):
                    qh, kt, off, _ = groups[g]
                    pe.wait_ge(S["e_done"], ONE + 2 * nb * it + (2 * g + p - 1 if g else 0))
                    diagonal = causal and kt * P >= qh * CHUNK
                    for n in range(2):
                        h = 2 * p + n
                        ins = pe.matmul(pair[p][:, n, off:], kst[l][st][0:BROWS, h, kt * P:(kt + 1) * P],
                                        qst[l][st][0:BROWS, h, qh * CHUNK + off:(qh + 1) * CHUNK],
                                        start=True, stop=not diagonal)
                        if diagonal:
                            ins = pe.matmul(pair[p][:, n, off:off + P], idb[:, :], lob[:, :], start=False, stop=True)
                    ins.then_inc(S["s_ready"], 1)

                def weigh_values(it, st, g):
                    qh, kt, off, last = groups[g]
                    pe.wait_ge(S["e_done"], ONE + 2 * nb * it + 2 * g + 2)
                    if kt == 0:
                        pe.wait_ge(S["cx"], ONE + 2 * it + qh)
                    for j in range(QUAD):
                        ins = pe.matmul(banks[RING][VW * j:VW * (j + 1), off:], vst[l][st][:, kt, VW * j:VW * (j + 1)],
                                        pr[:, g % 2, j, off:], start=kt == 0, stop=last)
                    ins.then_inc(S["pv_done"], 1)

                lead = LEAD[l]
                columns = [n for *_, n in units]
                widths = [CHUNK - off for _, _, off, _ in groups]

                def step_(it, st, loads, quads):
                    end = (lead, na, na + lead)[min(quads, 2)]
                    done, rows_group = [lead, 0], [0]

                    def tiles(g, share, most=3):
                        due = sum(columns) * (sum(widths[1:g]) + share * widths[g % nb]) / sum(widths)
                        for _ in range(most):
                            k = done[0]
                            if k == end or done[1] >= due or (k >= na and not rows_group[0] < 0):
                                break
                            if k < na:
                                ring_tile(it + 1, (st + 1) % NSTAGE, k)
                            else:
                                if k == na:
                                    pe.wait_ge(S[f"load{(st + 2) % NSTAGE}"], ONE + LOADS * DMA * loads)
                                ring_tile(it + 2, (st + 2) % NSTAGE, k - na)
                            if k == na - 1:
                                rows_group[0] = g + LAG
                            done[:] = k + 1, done[1] + columns[k % na]

                    for g in range(1, nb + 1):
                        for p in range(2):
                            if g < nb:
                                transposed_scores(it, st, g, p)
                            elif quads:
                                if p == 0:
                                    pe.wait_ge(S["mload"], ONE + 2 * DMA * (it + 2))
                                transposed_scores(it + 1, (st + 1) % NSTAGE, 0, p)
                            tiles(g, (p + 1) / 4)
                        if rows_group[0] == g:
                            maxima_rows(it + 1)
                            rows_group[0] = -1
                        weigh_values(it, st, g - 1)
                        tiles(g, 1)
                        if quads == 0 and g % 2 and 3 <= g < 3 + 2 * TT:
                            project_tile(l + 1, 0, (g - 3) // 2, True)
                    assert done[0] == end and (not quads or rows_group[0] < 0), (done, end)

                pe.wait_ge(F[l]["y_used"], ONE + TT * CHUNKS)
                maxima_rows(0)
                pe.wait_ge(S["load1"], ONE + LOADS * DMA)
                for k in range(RING):
                    ring_tile(1, 1, k)
                pe.wait_ge(s_ones, 2)
                pe.wait_ge(S["mload"], ONE + 2 * DMA)
                for p in range(2):
                    transposed_scores(0, 0, 0, p)
                for k in range(RING, lead):
                    ring_tile(1, 1, k)
                pe.wait_ge(s_ones, 4 + 3 * l)
                rounds = (STEPS - 2) // NSTAGE
                with pe.Fori(0, rounds) as u:
                    for r in range(NSTAGE):
                        step_(u * NSTAGE + r, r, u + 1 + (r + 2) // NSTAGE, 2)
                for it in range(rounds * NSTAGE, STEPS):
                    step_(it, it % NSTAGE, (it + 2) // NSTAGE + 1, STEPS - 1 - it)

            pe.wait_ge(s_cst, 2 * DMA)
            front(0)
            pe.wait_ge(F[0]["y_used"], ONE + TT * CHUNKS)
            pe.wait_ge(A[0]["load0"], ONE + LOADS * DMA)
            tables()
            pe.wait_ge(s_prep, 6)
            pe.wait_ge(D["wt_used"], ONE + 2 * KT * KT)
            pe.wait_ge(s_wo, 2 * DMA)
            attention(0)
            pe.wait_ge(s_w1, 3 * DMA)
            pe.wait_ge(A[0]["cx"], ONE + 2 * STEPS)
            front(1)
            attention(1)
            for i in range(1, CHUNKS):
                if i == 2:
                    pe.wait_ge(A[1]["cx"], ONE + 2 * STEPS)
                for t in range(TT):
                    project_tile(2, i, t)


def kernel(**inputs):
    import concourse.bacc as _bacc
    from concourse.bass_utils import run_bass_kernel_spmd as _run

    g = {k: np.asarray(v) for k, v in inputs.items()}
    c = np.ascontiguousarray
    lut4 = g["L1_ffn_lut4"].reshape(KT, 4, POS, GO, NIB).transpose(0, 2, 3, 1, 4)
    lut8 = g["L1_ffn_lut8"].reshape(KT, 4, POS, GO, NIB, NIB).transpose(0, 2, 3, 1, 4, 5)
    bd4 = np.zeros((KT, POS, GO, NIB, 4, POS, GO), np.float32)
    bd8 = np.zeros((KT, POS, GO, NIB, 4, GO, NIB), np.float32)
    for f in range(GO):
        bd8[:, :, f, :, :, f, :] = lut8[:, :, f].transpose(0, 1, 4, 2, 3)
        for pos in range(POS):
            bd4[:, pos, f, :, :, pos, f] = lut4[:, pos, f].transpose(0, 2, 1)
    tiles = lambda b: c(b[:2 * DIM].reshape(QKT, P).T)
    bqk1 = np.concatenate([g["L1_attn_bq"], g["L1_attn_bk"]])
    arrays = {
        "x": g["L0_attn_x"].reshape(TOK, DIM),
        "qkvw": g["L0_attn_attn_qkvw"],
        "bqk0": tiles(g["L0_attn_attn_qkvb"]),
        "bv0": c(g["L0_attn_attn_qkvb"][2 * DIM:]),
        "ow0": g["L0_attn_attn_ow"],
        "ob0": g["L0_attn_attn_ob"],
        "wbase": c(g["L0_ffn_W_base"].T),
        "bbase": g["L0_ffn_b_base"],
        "wrout": c(g["L0_ffn_W_router"].T),
        "brout": g["L0_ffn_b_router"],
        "lora_a": c(g["L0_ffn_lora_A"].transpose(1, 0, 2).reshape(DIM, EXPERTS * RANK)),
        "lora_b": g["L0_ffn_lora_B"].reshape(EXPERTS * RANK, DIM),
        "wq1": c(g["L1_attn_Wq"].T),
        "wk1": c(g["L1_attn_Wk"].T),
        "wv1": c(g["L1_attn_Wv"].T),
        "bqk1": tiles(bqk1),
        "bv1": g["L1_attn_bv"],
        "ow1": c(g["L1_attn_Wo"].T),
        "ob1": g["L1_attn_bo"],
        "qweight": c(g["L1_ffn_qweight"].transpose(1, 0, 2)),
        "bd4": bd4.reshape(KT * POS, P, 4, 32),
        "bd8": bd8.reshape(KT * POS, P, 4, P),
        "bffn": g["L1_ffn_bias"],
        "consts": constants(),
        "shifts": np.arange(BITS, dtype=np.int32),
    }
    nc = _bacc.Bacc("TRN2", target_bir_lowering=False, num_devices=1)
    args = [nc.dram_tensor(f"in_{n}", a.shape, mybir.dt.from_np(a.dtype), kind="ExternalInput").ap()
            for n, a in arrays.items()]
    args.append(nc.dram_tensor("out_0", (TOK, DIM), F32, kind="ExternalOutput").ap())
    program(nc, *args)
    r = _run(nc, [{f"in_{n}": c(a) for n, a in arrays.items()}], core_ids=[0])
    return r.results[0]["out_0"].reshape(BATCH, SEQ, DIM)
```
